# Optimizing a Trainium2 kernel written in Bass

```python
import numpy as np
import jax
import jax.numpy as jnp

def _softmax(x, axis=-1):
    return jax.nn.softmax(x, axis=axis)

def _gelu(x):
    return jax.nn.gelu(x, approximate=True)

def _silu(x):
    return jax.nn.silu(x)

def _sigmoid(x):
    return jax.nn.sigmoid(x)

def _layernorm(x, axis=-1, eps=1e-05):
    m = jnp.mean(x, axis=axis, keepdims=True)
    v = jnp.var(x, axis=axis, keepdims=True)
    return (x - m) / jnp.sqrt(v + eps)

def _scatter_add(tgt, idx, src, axis=0):
    return tgt.at[idx].add(src)

def _segment_sum(src, seg, n):
    return jax.ops.segment_sum(src, seg, n)
kernel_name = 'mk_gnn_resnorm_d1_gnn_r64_372df4'

def setup_inputs(seed: int=0):
    np.random.seed(seed)
    _w = jnp.asarray

    def _rec_inputs():
        import jax
        import jax.numpy as jnp
        _gk = jax.random.key(seed)
        x = -0.000202 + 1 * jax.random.normal(jax.random.fold_in(_gk, 1), (100000, 128), jnp.float32)
        src = jax.random.randint(jax.random.fold_in(_gk, 2), (25000,), 0, 100000, jnp.int32)
        dst = jax.random.randint(jax.random.fold_in(_gk, 3), (25000,), 0, 100000, jnp.int32)
        _o = jnp.argsort(dst, stable=True)
        src = src[_o]
        dst = dst[_o]
        edge_attr_3 = 0.00011001 + 1.00018 * jax.random.normal(jax.random.fold_in(_gk, 11), (25000, 3), jnp.float32)
        edge_weight1 = jax.random.uniform(jax.random.fold_in(_gk, 13), (25000, 1), jnp.float32, 0.0, 1)
        node_vec = jax.random.uniform(jax.random.fold_in(_gk, 14), (100000,), jnp.float32, 0.0, 0.999973)
        return (x, src, dst, edge_attr_3, edge_weight1, node_vec)
    x, src, dst, edge_attr_3, edge_weight1, node_vec = _rec_inputs()

    def _L0_gnn_setup():
        import jax, jax.numpy as jnp
        import numpy as np
        N_NODES = 50000
        N_EDGES = 25000
        HIDDEN = 128
        SPATIAL = 3
        SCORE_HIDDEN = 128
        EPS = 1e-12
        key = jax.random.key(seed)
        ks = jax.random.split(key, 12)
        s = 0.02
        return {'h': jax.random.normal(ks[0], (N_NODES, HIDDEN), dtype=jnp.float32), 'edge_index': jax.random.randint(ks[1], (2, N_EDGES), 0, N_NODES, dtype=jnp.int64), 'rel_pos': jax.random.normal(ks[2], (N_EDGES, SPATIAL), dtype=jnp.float32), 'distance': jax.random.uniform(ks[3], (N_EDGES, 1), dtype=jnp.float32), 'node_weight': jax.random.uniform(ks[4], (N_NODES,), dtype=jnp.float32), 'W1': jax.random.normal(ks[5], (2 * HIDDEN + SPATIAL + 1, SCORE_HIDDEN), dtype=jnp.float32) * s, 'b1': jnp.zeros((SCORE_HIDDEN,), dtype=jnp.float32), 'W2': jax.random.normal(ks[6], (SCORE_HIDDEN, SCORE_HIDDEN), dtype=jnp.float32) * s, 'b2': jnp.zeros((SCORE_HIDDEN,), dtype=jnp.float32), 'W3': jax.random.normal(ks[7], (SCORE_HIDDEN, 1), dtype=jnp.float32) * s, 'b3': jnp.zeros((1,), dtype=jnp.float32), 'Wv': jax.random.normal(ks[8], (HIDDEN, HIDDEN), dtype=jnp.float32) * s}
    _L0_gnn_all = _L0_gnn_setup()
    _L0_gnn_in = {k: v for k, v in _L0_gnn_all.items() if k in ('W1', 'b1', 'W2', 'b2', 'W3', 'b3', 'Wv')}
    del _L0_gnn_all
    return {'x': x, 'src': src, 'dst': dst, 'edge_attr_3': edge_attr_3, 'edge_weight1': edge_weight1, 'node_vec': node_vec, 'L0_gnn_W1': _L0_gnn_in['W1'], 'L0_gnn_b1': _L0_gnn_in['b1'], 'L0_gnn_W2': _L0_gnn_in['W2'], 'L0_gnn_b2': _L0_gnn_in['b2'], 'L0_gnn_W3': _L0_gnn_in['W3'], 'L0_gnn_b3': _L0_gnn_in['b3'], 'L0_gnn_Wv': _L0_gnn_in['Wv']}

def reference(x, src, dst, edge_attr_3, edge_weight1, node_vec, L0_gnn_W1, L0_gnn_b1, L0_gnn_W2, L0_gnn_b2, L0_gnn_W3, L0_gnn_b3, L0_gnn_Wv):
    import jax
    import jax.numpy as jnp

    def _L0_gnn_ref(h, edge_index, rel_pos, distance, node_weight, W1, b1, W2, b2, W3, b3, Wv):
        import jax, jax.numpy as jnp
        import numpy as np
        N_NODES = 50000
        N_EDGES = 25000
        HIDDEN = 128
        SPATIAL = 3
        SCORE_HIDDEN = 128
        EPS = 1e-12
        num_nodes = h.shape[0]
        dst, src = (edge_index[0], edge_index[1])
        edge_feat = jnp.concatenate([h[dst], h[src], rel_pos, distance], axis=-1)
        x = jax.nn.silu(edge_feat @ W1 + b1)
        x = jax.nn.silu(x @ W2 + b2)
        scores = (x @ W3 + b3)[:, 0]
        mx = jax.ops.segment_max(scores, dst, num_segments=num_nodes)
        exp_scores = jnp.exp(scores - mx[dst])
        den = jax.ops.segment_sum(exp_scores, dst, num_segments=num_nodes)
        alpha = exp_scores / (den[dst] + EPS)
        msg = h[src] @ Wv * (alpha * node_weight[src])[:, None]
        out = jax.ops.segment_sum(msg, dst, num_segments=num_nodes)
        return h + out
    edge_index = jnp.stack([src, dst])
    x = _layernorm(x + _L0_gnn_ref(x, edge_index, edge_attr_3, edge_weight1, node_vec, L0_gnn_W1, L0_gnn_b1, L0_gnn_W2, L0_gnn_b2, L0_gnn_W3, L0_gnn_b3, L0_gnn_Wv), axis=-1)
    return x

_drawn_inputs = setup_inputs


def setup_inputs(seed=0):
    import zlib

    import numpy as np

    out = dict(_drawn_inputs(seed))
    spreads = {'L0_gnn_b1': (0.0, 2.0), 'L0_gnn_b2': (0.0, 2.0)}
    factors = {'edge_attr_3': 25.245,
     'edge_weight1': 64.0,
     'node_vec': 3.821,
     'L0_gnn_W1': 8.0,
     'L0_gnn_W2': 22.713,
     'L0_gnn_W3': 8.0}
    for name, (base, spread) in spreads.items():
        noise = np.random.default_rng([zlib.crc32(name.encode()), seed]).standard_normal(out[name].shape)
        drawn = base * np.exp(spread * noise) if base else spread * noise
        out[name] = jnp.asarray(drawn.astype(out[name].dtype))
    for name, factor in factors.items():
        out[name] = (out[name] * factor).astype(out[name].dtype)
    return out
```

```python
from contextlib import ExitStack

import concourse.bass as bass
from concourse import mybir

F32 = mybir.dt.float32
BF16 = mybir.dt.bfloat16
I32 = mybir.dt.int32
ALU = mybir.AluOpType
ACT = mybir.ActivationFunctionType

P = 128
N = 100000
E = 25000
H = 128
TPG = 4
GE = TPG * P
G = -(-E // GE)
EP = G * GE
XW = H + 1
BR = 16
BN = P * BR
NB = -(-N // BN)
LASTROW = N - BN
RING = 4
ITERS = -(-(G + 3) // RING) * RING
ROUNDS = ITERS // RING
AHEAD = 2
RW = H + XW
XO = 2
T = G * TPG
CH = EP // 16
STEPS = 18
EPS_LN = 1e-5
EPS_DEN = 1e-12
FAR = -1.0e38
SKIP = float(1 << 20)
MAGIC = float(0x5F3759DF)
assert ITERS % RING == 0 and NB <= G


def gnn_kernel(nc, xw, snd_nat, rcv_nat, id_nat, key_row, iota, ef_t, w1, b1, w2, b2, w3, b3, wv, eye, out):
    far_d = nc.dram_tensor("far_d", (G, GE), BF16).ap()
    rec_d = nc.dram_tensor("rec_d", (EP, RW), F32).ap()
    srt_d = nc.dram_tensor("srt_d", (EP + 2, 2), F32).ap()
    with ExitStack() as ctx:
        def sb(name, shape, dt=F32):
            return ctx.enter_context(nc.sbuf_tensor(name, shape, dt))

        def ps(name, shape):
            return ctx.enter_context(nc.psum_tensor(name, shape, F32))

        def sem(name):
            return ctx.enter_context(nc.semaphore(name))

        ident = sb("ident", [P, P])
        nident = sb("nident", [P, P])
        ident16 = sb("ident16", [P, P], BF16)
        ones = sb("ones", [P, P])
        ones16 = sb("ones16", [3, GE], BF16)
        w1a = sb("w1a", [P, H])
        w1b = sb("w1b", [P, H])
        w1c = sb("w1c", [4, H])
        w2s = sb("w2s", [P, H])
        w2h = sb("w2h", [P, H])
        w3s = sb("w3s", [P, 1])
        w3h = sb("w3h", [P, 1])
        wvs = sb("wvs", [P, H])
        brow = sb("brow", [1, 3, H])
        brest = sb("brest", [1, 2, 3, H])
        bparts = sb("bparts", [1, 3, 3, H], BF16)
        bias3 = sb("bias3", [3, 3, H], BF16)
        snd_t = sb("snd_t", [P, T], I32)
        rcv_t = sb("rcv_t", [P, T], I32)
        keyid = sb("keyid", [P, T, 2])
        gidx_t = sb("gidx_t", [P, G, 2 * TPG], I32)
        srow = sb("srow", [P, 2, P, 2])
        nrow = sb("nrow", [P, 2, P, 2])
        key_s = sb("key_s", [P, T])
        next_s = sb("next_s", [P, T])
        id_s = sb("id_s", [P, T], I32)
        sidx_t = sb("sidx_t", [P, T], I32)
        key_g = sb("key_g", [G, GE + 1, 2])
        far_g = sb("far_g", [G, GE], BF16)
        halo = sb("halo", [1, 4])
        rank = sb("rank", [P, T])
        cnt_lt = sb("cnt_lt", [P, T])
        cnt_eq = sb("cnt_eq", [P, T])
        idrel = sb("idrel", [P, T])
        ranki = sb("ranki", [P, T], I32)
        sstage = sb("sstage", [P, TPG, 2])
        sistage = sb("sistage", [P, TPG], I32)
        gidx = sb("gidx", [P, RING, 2 * TPG], I32)
        ridx = sb("ridx", [P, RING, TPG], I32)
        sidx = sb("sidx", [P, RING, TPG], I32)
        hs = sb("hs", [P, RING, TPG, XW])
        rec = sb("rec", [P, RING, TPG, RW])
        back = sb("back", [P, RING, TPG, RW])
        ef = sb("ef", [4, RING, GE])
        far = sb("far", [P, RING, GE], BF16)
        res = sb("res", [P, RING, TPG, H])
        xin = sb("xin", [P, RING, BR, XW])
        xout = sb("xout", [P, XO, BR, H])
        hT = sb("hT", [P, 2, GE])
        th1 = sb("th1", [P, GE])
        x1 = sb("x1", [P, GE])
        th2 = sb("th2", [P, GE])
        x2 = sb("x2", [P, GE])
        mx = sb("mx", [P, 2, GE + 1])
        pa = sb("pa", [P, 2, 2, GE])
        den = sb("den", [P, 2, GE])
        z = sb("z", [P, 2, GE])
        v, y0, y1 = th1, x1, x2
        rden = sb("rden", [P, 2, TPG])
        st = sb("st", [P, 2, BR, 6])
        cw = sb("cw", [P, 6, BR])
        rs = sb("rs", [P, 2, 2, BR])

        p_hT = ps("p_hT", [P, 2, GE])
        p_1 = ps("p_1", [P, GE])
        p_2 = ps("p_2", [P, GE])
        p_dt = ps("p_dt", [P, 2, GE])
        p_w = ps("p_w", [P, GE])
        p_m = ps("p_m", [P, TPG, H])

        S = {n: sem(n) for n in (
            "w_in", "t_in", "far_out", "b_in", "setup", "consts_ready", "pool_turn",
            "chunk_in", "chunk_used", "slow", "rank_staged", "rank_scattered", "rank_free", "halo_ready", "halo_out",
            "sorted_done", "srt_in", "srt_T", "far_ready",
            "gidx_ready", "T_ready", "hT_ready", "mm1_done", "th1_ready", "x1_ready", "proj_ready", "rec_msg",
            "mm2_done", "th2_ready", "x2_ready", "s_ready", "rec_s", "rec_written",
            "ridx_ready", "sidx_ready", "sb_ready", "m_ready", "dt_ready", "pa_ready", "mT_ready",
            "v_ready", "z_ready", "agg_ready", "rden_ready", "y_done", "edge_stats", "chain2", "res_ready",
            "dense_stats", "chain1", "norm_done", "dense_written")}
        hs_in = [sem(f"hs_in{r}") for r in range(RING)]
        hk_in = [sem(f"hk_in{r}") for r in range(RING)]
        ef_in = [sem(f"ef_in{r}") for r in range(RING)]
        far_in = [sem(f"far_in{r}") for r in range(RING)]
        back_in = [sem(f"back_in{r}") for r in range(RING)]
        rec_out = [sem(f"rec_out{r}") for r in range(RING)]
        x_in = [sem(f"x_in{r}") for r in range(RING)]
        stored = [sem(f"stored{r}") for r in range(XO)]
        scattered = [sem(f"scattered{r}") for r in range(RING)]

        block = ctx.enter_context(nc.Block())

        class Turn:

            def __init__(self, k, u):
                self.k, self.u = k, u
                self.fixed = isinstance(k, int)

            def i(self, d=0):
                return self.k * RING + (self.u - d)

            def slot(self, d=0, n=RING):
                return (self.u - d) % n

            def live(self, d=0, count=G):
                return not self.fixed or 0 <= self.i(d) < count

        def wait(eng, s, t, d, per=1, off=0):
            if t.fixed and t.i(d) < 0:
                return
            eng.wait_ge(s, t.i(d) * per + (per + off))

        def wait_round(eng, sems, t, d, per):
            if t.fixed and t.i(d) < 0:
                return
            n = len(sems)
            eng.wait_ge(sems[t.slot(d, n)], t.k * (per * (RING // n)) + (((t.u - d) // n + 1) * per))

        def rounds(eng, body):
            for u in range(RING):
                body(Turn(0, u))
            with eng.Fori(1, ROUNDS - 2) as k:
                for u in range(RING):
                    body(Turn(k, u))
            for k in (ROUNDS - 2, ROUNDS - 1):
                for u in range(RING):
                    body(Turn(k, u))

        def column(table, g, fixed):
            return table[:, g * TPG:(g + 1) * TPG] if fixed else table[:, bass.ds(g * TPG, TPG)]

        xflat = xin[:].rearrange("p r b h -> p (r b h)")
        kb_i = xflat[:, 0:CH].bitcast(I32)
        kb = xflat[:, CH:2 * CH]
        jrow = xflat[:, 2 * CH:3 * CH]
        jm = xflat[:, 3 * CH:4 * CH]
        junk = xflat[:, 4 * CH:5 * CH]

        @block.sync
        def _(sp):
            for to, frm in ((snd_t[:], snd_nat), (rcv_t[:], rcv_nat), (idrel[:], id_nat)):
                sp.dma_start(to, frm).then_inc(S["t_in"], 16)
            for to, frm in ((ident[:], eye), (w1a[:], w1[0:H, :]), (w1b[:], w1[H:2 * H, :]), (w1c[:], w1[2 * H:, :]),
                            (w2s[:], w2), (w3s[:], w3), (wvs[:], wv), (brow[:, 0, :], b1), (brow[:, 1, :], b2),
                            (brow[:, 2, :], b3)):
                sp.dma_start(to, frm).then_inc(S["w_in"], 16)
            sp.wait_ge(S["consts_ready"], 1)
            sp.dma_start(bias3[:], bparts[:]).then_inc(S["b_in"], 16)
            sp.wait_ge(S["halo_ready"], 1)
            sp.dma_start(srt_d[0:1, :], halo[:, 0:2]).then_inc(S["halo_out"], 16)
            sp.dma_start(srt_d[EP + 1:EP + 2, :], halo[:, 2:4]).then_inc(S["halo_out"], 16)

            sp.dma_start(jrow, iota.to_broadcast((P, CH))).then_inc(S["chunk_in"], 16)
            with sp.Fori(0, EP // CH) as c:
                sp.wait_ge(S["chunk_used"], c + 1)
                sp.dma_start(kb_i, key_row[:, bass.ds(c * CH, CH)].to_broadcast((P, CH))).then_inc(S["chunk_in"], 16)
            sp.wait_ge(S["chunk_used"], EP // CH + 1)

            def rows_of(t, d):
                if t.fixed and t.i(d) == NB - 1:
                    return slice(LASTROW, N)
                return bass.ds(t.i(d) * BN, BN)

            def load_block(t, d):
                if not t.live(d, NB):
                    return
                if not t.fixed or t.i(d) >= RING:
                    wait(sp, S["norm_done"], t, d + RING)
                sp.dma_start(xin[:, t.slot(d)], xw[rows_of(t, d), :].rearrange("(p r) h -> p r h", p=P)
                             ).then_inc(x_in[t.slot(d)], 16)

            def load_ef(t, d):
                if not t.live(d, G):
                    return
                wait(sp, S["mm1_done"], t, d + RING)
                sp.dma_start(ef[:, t.slot(d), :], ef_t[:, bass.ds(t.i(d) * GE, GE)]).then_inc(ef_in[t.slot(d)], 16)

            for j in range(AHEAD):
                load_block(Turn(0, j), 0)
                load_ef(Turn(0, j), 0)

            def body(t):
                load_block(t, -AHEAD)
                load_ef(t, -AHEAD)
                if t.live(2):
                    wait(sp, S["rec_s"], t, 2)
                    wait(sp, S["rec_msg"], t, 2)
                    sp.dma_start(rec_d[bass.ds(t.i(2) * GE, GE), :].rearrange("(q p) w -> p q w", p=P),
                                 rec[:, t.slot(2)]).then_inc(rec_out[t.slot(2)], 16)
                if t.live(3, NB):
                    wait(sp, S["norm_done"], t, 3)
                    if t.fixed and t.i(3) == NB - 1:
                        wait_round(sp, stored, t, 4, 16)
                    sp.dma_start(out[rows_of(t, 3), :].rearrange("(p r) h -> p r h", p=P), xout[:, t.slot(3, XO)]
                                 ).then_inc(stored[t.slot(3, XO)], 16)

            rounds(sp, body)
            for r in range(XO):
                sp.wait_ge(stored[r], 16 * len(range(r, NB, XO)))
            sp.sem_inc(S["dense_written"], 1)
            for r in range(RING):
                sp.wait_ge(rec_out[r], 16 * len(range(r, G, RING)))
            sp.sem_inc(S["rec_written"], 1)

            sp.wait_ge(S["halo_out"], 32)
            sp.wait_ge(S["sorted_done"], 1)
            for to, first in ((srow, 1), (nrow, 2)):
                sp.dma_start(to[:, 0], srt_d[first:first + P * P, :].rearrange("(t p) w -> t p w", p=P)
                             ).then_inc(S["srt_in"], 16)
                sp.dma_start(to[0:T - P, 1], srt_d[first + P * P:first + EP, :].rearrange("(t p) w -> t p w", p=P)
                             ).then_inc(S["srt_in"], 16)
            sp.dma_start(key_g[:], bass.AP(tensor=srt_d.tensor, offset=0, ap=[[2 * GE, G], [1, 2 * (GE + 1)]])
                         ).then_inc(S["srt_in"], 16)
            sp.wait_ge(S["far_ready"], 1)
            sp.dma_start(far_d, far_g[:]).then_inc(S["far_out"], 16)
            sp.wait_ge(S["far_out"], 16)

            def load_far(t, d):
                if not t.live(d, G):
                    return
                wait(sp, S["m_ready"], t, d + RING)
                wait(sp, S["dt_ready"], t, d + RING)
                sp.dma_start(far[:, t.slot(d), :], far_d[bass.ds(t.i(d), 1), :].to_broadcast((P, GE))
                             ).then_inc(far_in[t.slot(d)], 16)

            for j in range(AHEAD):
                load_far(Turn(0, j), 0)
            rounds(sp, lambda t: load_far(t, -AHEAD))

        @block.gpsimd
        def _(pool):
            def rows_in(to, index, sems, r):
                for q in range(TPG):
                    pool.indirect_dma_start(out=to(q), out_offset=None, in_=xw,
                                            in_offset=bass.IndirectOffsetOnAxis(ap=index(q), axis=0)).then_inc(sems[r], 16)

            pool.sem_inc(S["rank_free"], 1)
            with pool.Fori(0, G) as g:
                pool.wait_ge(S["rank_staged"], g + 1)
                pool.sem_inc(S["pool_turn"], 1)
                for q in range(TPG):
                    pool.indirect_dma_start(out=srt_d, out_offset=bass.IndirectOffsetOnAxis(ap=sistage[:, q:q + 1], axis=0),
                                            in_=sstage[:, q, :], in_offset=None, bounds_check=EP, oob_is_err=False
                                            ).then_inc(S["rank_scattered"], 16)
                pool.wait_ge(S["rank_scattered"], (g + 1) * (16 * TPG))
                pool.sem_inc(S["rank_free"], 1)
            pool.wait_ge(S["rank_scattered"], 16 * TPG * G)
            pool.sem_inc(S["sorted_done"], 1)

            def gather(t, d):
                if not t.live(d, G):
                    return
                r = t.slot(d)
                wait(pool, S["gidx_ready"], t, d)
                wait(pool, S["T_ready"], t, d + RING)
                wait(pool, S["rec_msg"], t, d + RING)
                pool.sem_inc(S["pool_turn"], 1)
                rows_in(lambda q: hs[:, r, q, :], lambda q: gidx[:, r, TPG + q:TPG + q + 1], hs_in, r)
                wait_round(pool, rec_out, t, d + RING, 16)
                pool.sem_inc(S["pool_turn"], 1)
                rows_in(lambda q: rec[:, r, q, H:RW], lambda q: gidx[:, r, q:q + 1], hk_in, r)

            for j in range(AHEAD):
                gather(Turn(0, j), 0)
            rounds(pool, lambda t: gather(t, -AHEAD))

            def gather_back(t, d):
                if not t.live(d, G):
                    return
                r = t.slot(d)
                wait(pool, S["ridx_ready"], t, d)
                wait(pool, S["y_done"], t, d + RING, per=TPG)
                pool.sem_inc(S["pool_turn"], 1)
                for q in range(TPG):
                    pool.indirect_dma_start(
                        out=back[:, r, q, :], out_offset=None, in_=rec_d,
                        in_offset=bass.IndirectOffsetOnAxis(ap=ridx[:, r, q:q + 1], axis=0)).then_inc(back_in[r], 16)

            def scatter(t, d):
                if not t.live(d, G):
                    return
                r = t.slot(d)
                wait(pool, S["res_ready"], t, d)
                wait(pool, S["sidx_ready"], t, d)
                pool.sem_inc(S["pool_turn"], 1)
                for q in range(TPG):
                    pool.indirect_dma_start(
                        out=out, out_offset=bass.IndirectOffsetOnAxis(ap=sidx[:, r, q:q + 1], axis=0),
                        in_=res[:, r, q, :], in_offset=None, bounds_check=N - 1, oob_is_err=False
                    ).then_inc(scattered[r], 16)

            pool.wait_ge(S["rec_written"], 1)
            for j in range(AHEAD):
                gather_back(Turn(0, j), 0)
            pool.wait_ge(S["dense_written"], 1)

            def body2(t):
                gather_back(t, -AHEAD)
                scatter(t, 3)

            rounds(pool, body2)
            for r in range(RING):
                pool.wait_ge(scattered[r], 16 * TPG * len(range(r, G, RING)))

        @block.scalar
        def _(act):
            def dense_norm(t, d, lo, hi):
                if not t.live(d, NB):
                    return
                if lo == 0:
                    wait(act, S["chain1"], t, d, per=STEPS)
                    wait_round(act, stored, t, d + XO, 16)
                    wait_round(act, x_in, t, d, 16)
                for j in range(lo, hi):
                    ins = nc.scalar.activation(xout[:, t.slot(d, XO), j, :], xin[:, t.slot(d), j, 0:H], ACT.Identity,
                                               bias=rs[:, t.slot(d, 2), 1, j:j + 1], scale=rs[:, t.slot(d, 2), 0, j:j + 1])
                if hi == BR:
                    ins.then_inc(S["norm_done"], 1)

            def body(t):
                if t.live(1):
                    wait(act, S["mm2_done"], t, 1)
                    wait(act, S["x2_ready"], t, 2)
                    nc.scalar.activation(th2[:], p_2[:], ACT.Tanh, scale=0.5).then_inc(S["th2_ready"], 1)
                if t.live(0):
                    wait(act, S["T_ready"], t, 0)
                    wait(act, S["mm1_done"], t, 1)
                    wait(act, S["proj_ready"], t, 1)
                    nc.scalar.activation(hT[:], p_hT[:], ACT.Copy).then_inc(S["hT_ready"], 1)
                dense_norm(t, 2, 0, 4)
                if t.live(0):
                    wait(act, S["mm1_done"], t, 0)
                    wait(act, S["x1_ready"], t, 1)
                    nc.scalar.activation(th1[:], p_1[:], ACT.Tanh, scale=0.5).then_inc(S["th1_ready"], 1)
                dense_norm(t, 2, 4, BR)

            rounds(act, body)

            def body2(t):
                if t.live(0):
                    wait(act, S["dt_ready"], t, 0)
                    wait(act, S["z_ready"], t, 2)
                    nc.scalar.activation(pa[:, t.slot(0, 2)], p_dt[:], ACT.Exp).then_inc(S["pa_ready"], 1)

            rounds(act, body2)

        @block.tensor
        def _(pe):
            pe.wait_ge(S["w_in"], 160)
            pe.wait_ge(S["consts_ready"], 2)
            pe.wait_ge(S["b_in"], 16)

            def body(t):
                if t.live(1):
                    wait(pe, S["x1_ready"], t, 1)
                    wait(pe, S["x2_ready"], t, 2)
                    pe.matmul(p_2[:], w2h[:], x1[:], start=True, stop=False)
                    pe.matmul(p_2[:], bias3[:, 1, :], ones16[:], start=False, stop=True).then_inc(S["mm2_done"], 1)
                if t.live(0):
                    wait(pe, S["hT_ready"], t, 1)
                    wait_round(pe, hs_in, t, 0, 64)
                    for q in range(TPG):
                        pe.transpose(p_hT[:, 1, q * P:(q + 1) * P], hs[:, t.slot(), q, 0:H], ident[:])
                    wait_round(pe, hk_in, t, 0, 64)
                    for q in range(TPG):
                        ins = pe.transpose(p_hT[:, 0, q * P:(q + 1) * P], rec[:, t.slot(), q, H:2 * H], ident[:])
                    ins.then_inc(S["T_ready"], 1)
                if t.live(1):
                    wait(pe, S["x2_ready"], t, 1)
                    wait(pe, S["rec_s"], t, 2)
                    for q in range(TPG):
                        pe.matmul(p_w[:, q:q + 1], x2[:, q * P:(q + 1) * P], w3h[:], start=True, stop=False)
                        ins = pe.matmul(p_w[:, q:q + 1], ones16[:, 0:P], bias3[:, 2, 0:1], start=False, stop=True)
                    ins.then_inc(S["s_ready"], 1)
                if t.live(0):
                    wait(pe, S["hT_ready"], t, 0)
                    wait(pe, S["x1_ready"], t, 1)
                    wait_round(pe, ef_in, t, 0, 16)
                    pe.matmul(p_1[:], w1a[:], hT[:, 0, :], start=True, stop=False)
                    pe.matmul(p_1[:], w1b[:], hT[:, 1, :], start=False, stop=False)
                    pe.matmul(p_1[:], w1c[:], ef[:, t.slot(), :], start=False, stop=False)
                    pe.matmul(p_1[:], bias3[:, 0, :], ones16[:], start=False, stop=True).then_inc(S["mm1_done"], 1)
                    wait(pe, S["rec_msg"], t, 1)
                    for q in range(TPG):
                        ins = pe.matmul(p_m[:, q, :], hT[:, 1, q * P:(q + 1) * P], wvs[:], start=True, stop=True)
                    ins.then_inc(S["proj_ready"], 1)

            rounds(pe, body)

            pe.wait_ge(S["srt_in"], 80)
            pe.wait_ge(S["rec_s"], G)
            pe.wait_ge(S["x1_ready"], G)
            pe.wait_ge(S["hT_ready"], G)
            for n, (row, w, to) in enumerate(((srow, 0, p_hT[:, 0, :]), (nrow, 0, p_hT[:, 1, :]), (srow, 1, p_1[:]))):
                pe.transpose(to[:, 0:P], row[:, 0, :, w], ident[:])
                pe.transpose(to[:, P:T], row[0:T - P, 1, :, w], ident[0:T - P, 0:T - P]).then_inc(S["srt_T"], 1)

            def body2(t):
                if t.live(1):
                    wait_round(pe, back_in, t, 1, 64)
                    wait(pe, S["y_done"], t, 2, per=TPG)
                    for q in range(TPG):
                        ins = pe.transpose(p_w[:, q * P:(q + 1) * P], back[:, t.slot(1), q, 0:H], ident[:])
                    ins.then_inc(S["mT_ready"], 1)
                if t.live(0):
                    wait_round(pe, back_in, t, 0, 64)
                    wait(pe, S["pa_ready"], t, 1)
                    for q in range(TPG):
                        ins = pe.matmul(p_dt[:, 0, q * P:(q + 1) * P],
                                        back[:, t.slot(), q, RW - 1:RW].to_broadcast((P, P)), ident[:],
                                        start=(q == 0), stop=True, skip_group_check=True)
                    ins.then_inc(S["sb_ready"], 1)
                if t.live(1):
                    wait(pe, S["z_ready"], t, 1)
                    for q in range(TPG):
                        pe.matmul(p_2[:, q:q + 1], den[0:1, t.slot(1, 2), q * P:(q + 1) * P], ones[0:1, 0:1],
                                  start=True, stop=True)
                    for q in range(TPG):
                        ins = pe.transpose(p_m[:, q, :], z[:, t.slot(1, 2), q * P:(q + 1) * P], ident[:])
                    ins.then_inc(S["agg_ready"], 1)
                if t.live(0):
                    wait(pe, S["m_ready"], t, 0)
                    wait_round(pe, far_in, t, 0, 16)
                    m = mx[:, t.slot(0, 2), :]
                    pe.matmul(p_dt[:, 0, :], nident[:], m[:, 1:GE + 1], start=False, stop=True, skip_group_check=True)
                    pe.matmul(p_dt[:, 1, :], ident16[:], far[:, t.slot(), :], start=True, stop=False)
                    pe.matmul(p_dt[:, 1, :], ident[:], m[:, 0:GE], start=False, stop=False)
                    pe.matmul(p_dt[:, 1, :], nident[:], m[:, 1:GE + 1], start=False, stop=True).then_inc(S["dt_ready"], 1)

            rounds(pe, body2)

        @block.vector
        def _(dve):
            vec = nc.vector
            count = [0]

            def link(ins, s="setup"):
                count[0] += 1
                ins.then_inc(S[s], 1)
                dve.wait_ge(S[s], count[0])

            dve.wait_ge(S["t_in"], 48)
            vec.tensor_scalar(gidx_t[:, :, 0:TPG], rcv_t[:].rearrange("p (g q) -> p g q", q=TPG), float(N - 1), None, ALU.min)
            vec.tensor_copy(gidx_t[:, :, TPG:2 * TPG], snd_t[:].rearrange("p (g q) -> p g q", q=TPG))
            vec.tensor_copy(keyid[:, :, 0], rcv_t[:])
            vec.tensor_copy(keyid[:, :, 1], idrel[:])
            vec.memset(rank[:], 1.0)
            vec.memset(cnt_lt[:], 0.0)
            vec.memset(cnt_eq[:], 0.0)
            vec.memset(halo[:, 0:2], -1.0)
            link(vec.memset(halo[:, 2:4], float(N + 1)))
            vec.memset(ones[:], 1.0).then_inc(S["halo_ready"], 1)
            vec.memset(mx[:, 0, 0:1], 0.0)
            vec.memset(den[:, 1, GE - 1:GE], 0.0)
            vec.memset(z[:, 1, GE - 1:GE], 0.0)
            vec.memset(ones16[:], 1.0)
            dve.wait_ge(S["w_in"], 160)
            vec.tensor_scalar(nident[:], ident[:], -1.0, None, ALU.mult)
            vec.tensor_copy(ident16[:], ident[:])
            vec.tensor_scalar(w2h[:], w2s[:], 0.5, None, ALU.mult)
            vec.tensor_scalar(w3h[:], w3s[:], 0.5, None, ALU.mult)
            link(vec.tensor_copy(bparts[:, 0], brow[:]))
            link(vec.tensor_tensor(brest[:, 0], brow[:], bparts[:, 0], ALU.subtract))
            link(vec.tensor_copy(bparts[:, 1], brest[:, 0]))
            link(vec.tensor_tensor(brest[:, 1], brest[:, 0], bparts[:, 1], ALU.subtract))
            link(vec.tensor_copy(bparts[:, 2], brest[:, 1]))
            link(vec.memset(cw[:], 1.0))
            link(vec.memset(cw[:, 0, 0:1], 1.0))
            vec.memset(cw[:, 0, 0:1], 1.0).then_inc(S["consts_ready"], 2)

            vec.memset(junk, 0.0).then_inc(S["chunk_used"], 1)
            per = 3 + 3 * T
            with dve.Fori(0, EP // CH) as c:
                dve.wait_ge(S["chunk_in"], c * 16 + 32)
                vec.tensor_copy(kb, kb_i).then_inc(S["slow"], 1)
                dve.wait_ge(S["slow"], c * per + 1)
                vec.memset(cw[:, 0, 1:2], 1.0)
                with dve.Fori(0, T) as t:
                    base = c * per + t * 3 + 1
                    key = keyid[:, bass.ds(t, 1), 0]
                    vec.tensor_scalar(junk, kb, key, 0.0, ALU.is_lt, ALU.add, accum_out=cnt_lt[:, bass.ds(t, 1)])
                    vec.tensor_scalar(jm, jrow, idrel[:, bass.ds(t, 1)], None, ALU.is_lt).then_inc(S["slow"], 1)
                    dve.wait_ge(S["slow"], base + 1)
                    vec.scalar_tensor_tensor(out=junk, in0=kb, scalar=key, in1=jm, op0=ALU.is_equal, op1=ALU.mult
                                             ).then_inc(S["slow"], 1)
                    dve.wait_ge(S["slow"], base + 2)
                    vec.tensor_reduce(cnt_eq[:, bass.ds(t, 1)], junk, mybir.AxisListType.X, ALU.add).then_inc(S["slow"], 1)
                    dve.wait_ge(S["slow"], base + 3)
                vec.tensor_tensor(rank[:], rank[:], cnt_lt[:], ALU.add).then_inc(S["slow"], 1)
                dve.wait_ge(S["slow"], c * per + (3 * T + 2))
                vec.tensor_scalar(idrel[:], idrel[:], -float(CH), None, ALU.add)
                vec.tensor_tensor(rank[:], rank[:], cnt_eq[:], ALU.add).then_inc(S["slow"], 1)
                dve.wait_ge(S["slow"], c * per + (3 * T + 3))
                vec.memset(cw[:, 0, 0:1], 1.0).then_inc(S["chunk_used"], 1)
            link(vec.tensor_copy(ranki[:], rank[:]))
            with dve.Fori(0, G) as g:
                with_g = bass.ds(g * TPG, TPG)
                dve.wait_ge(S["rank_free"], g + 1)
                vec.tensor_copy(sistage[:], ranki[:, with_g])
                vec.tensor_copy(sstage[:], keyid[:, with_g, :]).then_inc(S["rank_staged"], 1)

            def copy_gidx(t, d):
                if t.live(d, G):
                    wait_round(dve, hk_in, t, d + RING, 64)
                    wait_round(dve, hs_in, t, d + RING, 64)
                    g = t.i(d)
                    at = gidx_t[:, g, :] if t.fixed else gidx_t[:, bass.ds(g, 1), :].rearrange("p a q -> p (a q)")
                    vec.tensor_copy(gidx[:, t.slot(d), :], at).then_inc(S["gidx_ready"], 1)

            for j in range(AHEAD):
                copy_gidx(Turn(0, j), 0)

            def chain(t, d, n, s, o, step_sem, stats_sem, gate):
                sm, dl, q, va, a, b = (cw[:, m, 0:n] for m in range(6))
                r, bi = o[:, 0, 0:n], o[:, 1, 0:n]
                ri, vi, ai = r.bitcast(I32), va.bitcast(I32), a.bitcast(I32)
                s = s[:, 0:n, :]

                def step(ins):
                    ins.then_inc(step_sem, 1)

                def after(m):
                    wait(dve, step_sem, t, d, per=STEPS, off=m - STEPS)

                wait(dve, stats_sem, t, d)
                step(vec.tensor_tensor(dl, s[:, :, 1], s[:, :, 4], ALU.subtract)); yield
                step(vec.tensor_tensor(sm, s[:, :, 1], s[:, :, 4], ALU.add)); yield
                step(vec.tensor_tensor(q, s[:, :, 2], s[:, :, 5], ALU.add)); yield
                after(1)
                step(vec.tensor_tensor(a, dl, dl, ALU.mult)); yield
                after(4)
                step(vec.scalar_tensor_tensor(out=b, in0=a, scalar=32.0, in1=q, op0=ALU.mult, op1=ALU.add)); yield
                after(5)
                step(vec.tensor_scalar(va, b, 1.0 / H, EPS_LN / 4, ALU.mult, ALU.add)); yield
                after(6)
                step(vec.tensor_scalar(ai, vi, 1, None, ALU.logical_shift_right)); yield
                after(7)
                gate()
                step(vec.tensor_scalar(ri, ai, -1.0, MAGIC, ALU.mult, ALU.add)); yield
                for m in range(3):
                    after(8 + 3 * m)
                    step(vec.scalar_tensor_tensor(out=a, in0=r, scalar=-0.5, in1=r, op0=ALU.mult, op1=ALU.mult)); yield
                    after(9 + 3 * m)
                    step(vec.tensor_tensor(b, a, va, ALU.mult)); yield
                    after(10 + 3 * m)
                    step(vec.scalar_tensor_tensor(out=r, in0=b, scalar=1.5, in1=r, op0=ALU.add, op1=ALU.mult)); yield
                after(17)
                step(vec.scalar_tensor_tensor(out=bi, in0=sm, scalar=-0.5, in1=r, op0=ALU.mult, op1=ALU.mult)); yield
                after(18)

            def body(t):
                def gate():
                    if t.live(3, NB):
                        wait(dve, S["norm_done"], t, 3)

                steps = iter(())
                if t.live(1, NB):
                    steps = chain(t, 1, BR, st[:, t.slot(1, 2)], rs[:, t.slot(1, 2)], S["chain1"], S["dense_stats"], gate)

                def more(n=1):
                    for _ in range(n):
                        next(steps, None)

                def stats(lo, hi):
                    if not t.live(0, NB):
                        return
                    if lo == 0:
                        wait_round(dve, x_in, t, 0, 16)
                    for j in range(lo, hi):
                        ins = vec.bn_stats(st[:, t.slot(0, 2), j, :], xin[:, t.slot(), j, 0:H])
                        if j == BR - 1:
                            ins.then_inc(S["dense_stats"], 1)
                        more()

                copy_gidx(t, -AHEAD)
                stats(0, 4)
                if t.live(1):
                    wait(dve, S["th2_ready"], t, 1)
                    wait(dve, S["s_ready"], t, 2)
                    vec.scalar_tensor_tensor(out=x2[:], in0=th2[:], scalar=1.0, in1=p_2[:], op0=ALU.add, op1=ALU.mult
                                             ).then_inc(S["x2_ready"], 1)
                more()
                stats(4, 10)
                if t.live(0):
                    wait(dve, S["th1_ready"], t, 0)
                    wait(dve, S["mm2_done"], t, 1)
                    vec.scalar_tensor_tensor(out=x1[:], in0=th1[:], scalar=1.0, in1=p_1[:], op0=ALU.add, op1=ALU.mult
                                             ).then_inc(S["x1_ready"], 1)
                more()
                if t.live(1):
                    wait(dve, S["s_ready"], t, 1)
                    vec.tensor_copy(rec[:, t.slot(1), :, RW - 1], p_w[:, 0:TPG]).then_inc(S["rec_s"], 1)
                stats(10, BR)
                if t.live(0):
                    wait(dve, S["proj_ready"], t, 0)
                    wait_round(dve, rec_out, t, RING, 16)
                    w = hs[:, t.slot(), :, H:H + 1].to_broadcast((P, TPG, H))
                    vec.tensor_tensor(rec[:, t.slot(), :, 0:H], p_m[:], w, ALU.mult).then_inc(S["rec_msg"], 1)
                more(99)

            rounds(dve, body)

            n0 = count[0]
            dve.wait_ge(S["srt_in"], 80)
            link(vec.tensor_tensor(far_g[:], key_g[:, 1:GE + 1, 0], key_g[:, 0:GE, 0], ALU.not_equal))
            link(vec.tensor_scalar(far_g[:], far_g[:], FAR, None, ALU.mult))
            vec.memset(cw[:, 0, 0:1], 1.0).then_inc(S["far_ready"], 1)
            dve.wait_ge(S["srt_T"], 3)
            vec.tensor_copy(id_s[:], p_1[:, 0:T])
            link(vec.tensor_copy(key_s[:], p_hT[:, 0, 0:T]))
            link(vec.tensor_tensor(next_s[:], key_s[:], p_hT[:, 1, 0:T], ALU.is_equal))
            link(vec.scalar_tensor_tensor(out=sidx_t[:], in0=next_s[:], scalar=SKIP, in1=key_s[:], op0=ALU.mult, op1=ALU.add))

            def copy_ridx(t, d):
                if t.live(d, G):
                    wait_round(dve, back_in, t, d + RING, 64)
                    vec.tensor_copy(ridx[:, t.slot(d), :], column(id_s, t.i(d), t.fixed)).then_inc(S["ridx_ready"], 1)

            for j in range(AHEAD):
                copy_ridx(Turn(0, j), 0)
            yb = [y0, y1]

            def body2(t):
                steps = iter(())
                if t.live(2):
                    steps = chain(t, 2, TPG, st[:, t.slot(2, 2)], rs[:, t.slot(2, 2)], S["chain2"], S["edge_stats"],
                                  lambda: None)

                def more(n=1):
                    for _ in range(n):
                        next(steps, None)

                copy_ridx(t, -AHEAD)
                more()
                if t.live(1):
                    pp = pa[:, t.slot(1, 2)]
                    wait(dve, S["pa_ready"], t, 1)
                    wait(dve, S["agg_ready"], t, 3)
                    vec.tensor_tensor_scan(den[:, t.slot(1, 2), :], pp[:, 1, :], pp[:, 0, :],
                                           den[:, t.slot(2, 2), GE - 1:GE], ALU.mult, ALU.add)
                    more(2)
                    wait(dve, S["mT_ready"], t, 1)
                    vec.tensor_tensor(v[:], pp[:, 0, :], p_w[:], ALU.mult).then_inc(S["v_ready"], 1)
                    more(3)
                    wait(dve, S["v_ready"], t, 1)
                    vec.tensor_tensor_scan(z[:, t.slot(1, 2), :], pp[:, 1, :], v[:], z[:, t.slot(2, 2), GE - 1:GE],
                                           ALU.mult, ALU.add).then_inc(S["z_ready"], 1)
                    more(2)
                if t.live(0):
                    m = mx[:, t.slot(0, 2), :]
                    wait(dve, S["sb_ready"], t, 0)
                    wait(dve, S["dt_ready"], t, 2)
                    wait_round(dve, far_in, t, 0, 16)
                    if not (t.fixed and t.i(0) == 0):
                        vec.tensor_copy(m[:, 0:1], mx[:, t.slot(1, 2), GE:GE + 1])
                    vec.tensor_tensor_scan(m[:, 1:GE + 1], far[:, t.slot(), :], p_dt[:, 0, :],
                                           0.0 if t.fixed and t.i(0) == 0 else mx[:, t.slot(1, 2), GE:GE + 1],
                                           ALU.add, ALU.max).then_inc(S["m_ready"], 1)
                    more(4)
                if t.live(1):
                    wait(dve, S["agg_ready"], t, 1)
                    vec.tensor_scalar(rden[:, 0, :], p_2[:, 0:TPG], 2.0, 2 * EPS_DEN, ALU.mult, ALU.add
                                      ).then_inc(S["rden_ready"], 1)
                    more(1)
                    wait(dve, S["rden_ready"], t, 1, per=2, off=-1)
                    vec.reciprocal(rden[:, 1, :], rden[:, 0, :]).then_inc(S["rden_ready"], 1)
                    more(1)
                    wait(dve, S["rden_ready"], t, 1, per=2)
                    for q in range(TPG):
                        vec.scalar_tensor_tensor(out=yb[t.slot(1, 2)][:, q * H:(q + 1) * H], in0=p_m[:, q, :],
                                                 scalar=rden[:, 1, q:q + 1], in1=back[:, t.slot(1), q, H:2 * H],
                                                 op0=ALU.mult, op1=ALU.add).then_inc(S["y_done"], 1)
                        more(1)
                    for q in range(TPG):
                        wait(dve, S["y_done"], t, 1, per=TPG, off=q + 1 - TPG)
                        ins = vec.bn_stats(st[:, t.slot(1, 2), q, :], yb[t.slot(1, 2)][:, q * H:(q + 1) * H])
                        more(1)
                    ins.then_inc(S["edge_stats"], 1)
                more(99)
                if t.live(2):
                    wait_round(dve, scattered, t, 2 + RING, 64)
                    for q in range(TPG):
                        ins = vec.tensor_scalar(res[:, t.slot(2), q, :], yb[t.slot(2, 2)][:, q * H:(q + 1) * H],
                                                rs[:, t.slot(2, 2), 0, q:q + 1],
                                                rs[:, t.slot(2, 2), 1, q:q + 1], ALU.mult, ALU.add)
                    ins.then_inc(S["res_ready"], 1)
                    vec.tensor_copy(sidx[:, t.slot(2), :], column(sidx_t, t.i(2), t.fixed)).then_inc(S["sidx_ready"], 1)

            rounds(dve, body2)


def kernel(x, src, dst, edge_attr_3, edge_weight1, node_vec, L0_gnn_W1, L0_gnn_b1, L0_gnn_W2, L0_gnn_b2, L0_gnn_W3,
           L0_gnn_b3, L0_gnn_Wv):
    import numpy as np
    import concourse.bacc as bacc
    from concourse import mybir as mb
    from concourse.bass_utils import run_bass_kernel_spmd

    src = np.asarray(src)
    dst = np.asarray(dst)
    rcv = np.full(EP, N, src.dtype)
    rcv[:E] = src
    snd = np.zeros(EP, dst.dtype)
    snd[:E] = dst
    ef = np.zeros((4, EP), np.float32)
    ef[0:3, :E] = np.asarray(edge_attr_3).T
    ef[3, :E] = np.asarray(edge_weight1)[:, 0]

    def nat(a):
        return np.ascontiguousarray(a.reshape(G * TPG, P).T)

    arrays = {
        "xw": np.concatenate([np.asarray(x), np.asarray(node_vec)[:, None]], axis=1),
        "snd_nat": nat(snd),
        "rcv_nat": nat(rcv),
        "id_nat": nat(np.arange(EP, dtype=np.float32)),
        "key_row": rcv.reshape(1, EP),
        "iota": np.arange(CH, dtype=np.float32).reshape(1, CH),
        "ef_t": ef,
        "w1": np.asarray(L0_gnn_W1),
        "b1": np.asarray(L0_gnn_b1).reshape(1, H),
        "w2": np.asarray(L0_gnn_W2),
        "b2": np.asarray(L0_gnn_b2).reshape(1, H),
        "w3": np.asarray(L0_gnn_W3),
        "b3": np.ascontiguousarray(np.broadcast_to(np.asarray(L0_gnn_b3).reshape(1, 1), (1, H))),
        "wv": np.asarray(L0_gnn_Wv),
        "eye": np.eye(P, dtype=np.float32),
    }
    nc = bacc.Bacc("TRN2", target_bir_lowering=False, num_devices=1)
    feed, args = {}, []
    for name, a in arrays.items():
        a = np.ascontiguousarray(a)
        feed[f"in_{name}"] = a
        args.append(nc.dram_tensor(f"in_{name}", a.shape, mb.dt.from_np(a.dtype), kind="ExternalInput").ap())
    out = nc.dram_tensor("out_rows", (N, H), mb.dt.float32, kind="ExternalOutput").ap()
    gnn_kernel(nc, *args, out)
    r = run_bass_kernel_spmd(nc, [feed], core_ids=[0])
    return r.results[0]["out_rows"]
```

```python
from contextlib import ExitStack

import concourse.bass as bass
from concourse import mybir

F32 = mybir.dt.float32
BF16 = mybir.dt.bfloat16
I32 = mybir.dt.int32
ALU = mybir.AluOpType
ACT = mybir.ActivationFunctionType

P = 128
N = 100000
E = 25000
H = 128
TPG = 4
GE = TPG * P
G = -(-E // GE)
EP = G * GE
XW = H + 1
BR = 16
BN = P * BR
NB = -(-N // BN)
LASTROW = N - BN
RING = 4
ITERS = -(-(G + 3) // RING) * RING
ROUNDS = ITERS // RING
AHEAD = 2
RW = H + XW
XO = 2
T = G * TPG
CH = EP // 16
ROWLEN = EP // P
BUCKET = 1024
CAP = 384
SORTW = 512
PITCH = 1024
PAD = 256
NEAR = 3
BIG = 1.0e9
STEPS = 18
EPS_LN = 1e-5
EPS_DEN = 1e-12
FAR = -1.0e38
SKIP = float(1 << 20)
MAGIC = float(0x5F3759DF)
assert ITERS % RING == 0 and NB <= G


def gnn_kernel(nc, xw, snd_nat, rcv_nat, id_nat, key_row, iota, tri, ef_t, w1, b1, w2, b2, w3, b3, wv, eye, out):
    far_d = nc.dram_tensor("far_d", (G, GE), BF16).ap()
    rec_d = nc.dram_tensor("rec_d", (EP, RW), F32).ap()
    srt_d = nc.dram_tensor("srt_d", (EP + 2, 2), F32).ap()
    buckets_d = nc.dram_tensor("buckets_d", (P, PITCH), F32).ap()
    with ExitStack() as ctx:
        def sb(name, shape, dt=F32):
            return ctx.enter_context(nc.sbuf_tensor(name, shape, dt))

        def ps(name, shape):
            return ctx.enter_context(nc.psum_tensor(name, shape, F32))

        def sem(name):
            return ctx.enter_context(nc.semaphore(name))

        ident = sb("ident", [P, P])
        nident = sb("nident", [P, P])
        ident16 = sb("ident16", [P, P], BF16)
        ones = sb("ones", [P, P])
        ones16 = sb("ones16", [3, GE], BF16)
        w1a = sb("w1a", [P, H])
        w1b = sb("w1b", [P, H])
        w1c = sb("w1c", [4, H])
        w2s = sb("w2s", [P, H])
        w2h = sb("w2h", [P, H])
        w3s = sb("w3s", [P, 1])
        w3h = sb("w3h", [P, 1])
        wvs = sb("wvs", [P, H])
        brow = sb("brow", [1, 3, H])
        brest = sb("brest", [1, 2, 3, H])
        bparts = sb("bparts", [1, 3, 3, H], BF16)
        bias3 = sb("bias3", [3, 3, H], BF16)
        snd_t = sb("snd_t", [P, T], I32)
        rcv_t = sb("rcv_t", [P, T], I32)
        keyid = sb("keyid", [P, T, 2])
        gidx_t = sb("gidx_t", [P, G, 2 * TPG], I32)
        srow = sb("srow", [P, 2, P, 2])
        nrow = sb("nrow", [P, 2, P, 2])
        key_s = sb("key_s", [P, T])
        next_s = sb("next_s", [P, T])
        id_s = sb("id_s", [P, T], I32)
        sidx_t = sb("sidx_t", [P, T], I32)
        key_g = sb("key_g", [G, GE + 1, 2])
        far_g = sb("far_g", [G, GE], BF16)
        halo = sb("halo", [1, 4])
        rank = sb("rank", [P, T])
        cnt_lt = sb("cnt_lt", [P, T])
        cnt_eq = sb("cnt_eq", [P, T])
        idrel = sb("idrel", [P, T])
        ranki = sb("ranki", [P, T], I32)
        sstage = sb("sstage", [P, TPG, 2])
        sistage = sb("sistage", [P, TPG], I32)
        gidx = sb("gidx", [P, RING, 2 * TPG], I32)
        ridx = sb("ridx", [P, RING, TPG], I32)
        sidx = sb("sidx", [P, RING, TPG], I32)
        hs = sb("hs", [P, RING, TPG, XW])
        rec = sb("rec", [P, RING, TPG, RW])
        back = sb("back", [P, RING, TPG, RW])
        ef = sb("ef", [4, RING, GE])
        far = sb("far", [P, RING, GE], BF16)
        res = sb("res", [P, RING, TPG, H])
        xin = sb("xin", [P, RING, BR, XW])
        xout = sb("xout", [P, XO, BR, H])
        hT = sb("hT", [P, 2, GE])
        th1 = sb("th1", [P, GE])
        x1 = sb("x1", [P, GE])
        th2 = sb("th2", [P, GE])
        x2 = sb("x2", [P, GE])
        shared = sb("shared", [P, 6912])
        at = [0]

        def part(size):
            at[0] += size
            return shared[:, at[0] - size:at[0]]

        mx = part(2 * (GE + 1)).rearrange("p (r e) -> p r e", r=2)
        pa = part(4 * GE).rearrange("p (r a e) -> p r a e", r=2, a=2)
        den = part(2 * GE).rearrange("p (r e) -> p r e", r=2)
        z = part(2 * GE).rearrange("p (r e) -> p r e", r=2)
        at[0] = 0
        hot = part(2 * GE).rearrange("p (r q b) -> p r q b", r=2, q=TPG)
        hot16 = part(GE).bitcast(BF16).rearrange("p (r q b) -> p r q b", r=2, q=TPG)
        placed = part(TPG * CAP).rearrange("p (q c) -> p q c", q=TPG)
        bucket = part(PITCH)
        other = part(SORTW)
        pick = part(NEAR * ROWLEN).rearrange("p (n j) -> p n j", n=NEAR)
        srt = part(2 * ROWLEN).rearrange("p (j w) -> p j w", w=2)
        counts = part(P)
        incl = part(P)
        small = part(P)
        bno = sb("bno", [P, T])
        junk16 = sb("junk16", [P, TPG, P])
        comp = sb("comp", [P, T])
        pos = sb("pos", [P, 2, TPG])
        slot_no = sb("slot_no", [P, CAP])
        before16 = sb("before16", [P, P], BF16)
        after16 = sb("after16", [P, P], BF16)
        all16 = sb("all16", [P, P], BF16)
        cols = sb("cols", [P, 16])
        picki = sb("picki", [P, NEAR], I32)
        flag = sb("flag", [P, 1], I32)
        q_i = sb("q_i", [P, T], I32)
        v, y0, y1 = th1, x1, x2
        rden = sb("rden", [P, 2, TPG])
        st = sb("st", [P, 2, BR, 6])
        cw = sb("cw", [P, 6, BR])
        rs = sb("rs", [P, 2, 2, BR])

        p_hT = ps("p_hT", [P, 2, GE])
        p_1 = ps("p_1", [P, GE])
        p_2 = ps("p_2", [P, GE])
        p_dt = ps("p_dt", [P, 2, GE])
        p_w = ps("p_w", [P, GE])
        p_m = ps("p_m", [P, TPG, H])

        S = {n: sem(n) for n in (
            "w_in", "t_in", "far_out", "b_in", "setup", "consts_ready", "pool_turn",
            "chunk_in", "chunk_used", "slow", "rank_staged", "rank_scattered", "rank_free", "halo_ready", "halo_out",
            "hot_ready", "cnt_ready", "pos_ready", "placed_ready", "place_done", "buckets_ready", "count_row", "count_col",
            "viol", "viol_sum", "flag_ready", "bucket_out", "pick_ready", "picked", "srt_ready", "srt_out", "sdve",
            "sorted_done", "srt_in", "srt_T", "far_ready",
            "tables_ready", "gidx_ready", "T_ready", "hT_ready", "mm1_done", "th1_ready", "x1_ready", "proj_ready", "rec_msg",
            "mm2_done", "th2_ready", "x2_ready", "s_ready", "rec_s", "rec_written",
            "ridx_ready", "sidx_ready", "sb_ready", "m_ready", "dt_ready", "pa_ready", "mT_ready",
            "v_ready", "z_ready", "agg_ready", "rden_ready", "y_done", "edge_stats", "chain2", "res_ready",
            "dense_stats", "chain1", "norm_done", "dense_written")}
        hs_in = [sem(f"hs_in{r}") for r in range(RING)]
        hk_in = [sem(f"hk_in{r}") for r in range(RING)]
        ef_in = [sem(f"ef_in{r}") for r in range(RING)]
        far_in = [sem(f"far_in{r}") for r in range(RING)]
        back_in = [sem(f"back_in{r}") for r in range(RING)]
        rec_out = [sem(f"rec_out{r}") for r in range(RING)]
        x_in = [sem(f"x_in{r}") for r in range(RING)]
        stored = [sem(f"stored{r}") for r in range(XO)]
        scattered = [sem(f"scattered{r}") for r in range(RING)]

        block = ctx.enter_context(nc.Block())

        class Turn:

            def __init__(self, k, u):
                self.k, self.u = k, u
                self.fixed = isinstance(k, int)

            def i(self, d=0):
                return self.k * RING + (self.u - d)

            def slot(self, d=0, n=RING):
                return (self.u - d) % n

            def live(self, d=0, count=G):
                return not self.fixed or 0 <= self.i(d) < count

        def wait(eng, s, t, d, per=1, off=0):
            if t.fixed and t.i(d) < 0:
                return
            eng.wait_ge(s, t.i(d) * per + (per + off))

        def wait_round(eng, sems, t, d, per):
            if t.fixed and t.i(d) < 0:
                return
            n = len(sems)
            eng.wait_ge(sems[t.slot(d, n)], t.k * (per * (RING // n)) + (((t.u - d) // n + 1) * per))

        def rounds(eng, body):
            for u in range(RING):
                body(Turn(0, u))
            with eng.Fori(1, ROUNDS - 2) as k:
                for u in range(RING):
                    body(Turn(k, u))
            for k in (ROUNDS - 2, ROUNDS - 1):
                for u in range(RING):
                    body(Turn(k, u))

        def column(table, g, fixed):
            return table[:, g * TPG:(g + 1) * TPG] if fixed else table[:, bass.ds(g * TPG, TPG)]

        xflat = xin[:].rearrange("p r b h -> p (r b h)")
        kb_i = xflat[:, 0:CH].bitcast(I32)
        kb = xflat[:, CH:2 * CH]
        jrow = xflat[:, 2 * CH:3 * CH]
        jm = xflat[:, 3 * CH:4 * CH]
        junk = xflat[:, 4 * CH:5 * CH]

        @block.sync
        def _(sp):
            for to, frm in ((snd_t[:], snd_nat), (rcv_t[:], rcv_nat), (idrel[:], id_nat)):
                sp.dma_start(to, frm).then_inc(S["t_in"], 16)
            for to, frm in ((ident[:], eye), (w1a[:], w1[0:H, :]), (w1b[:], w1[H:2 * H, :]), (w1c[:], w1[2 * H:, :]),
                            (w2s[:], w2), (w3s[:], w3), (wvs[:], wv), (brow[:, 0, :], b1), (brow[:, 1, :], b2),
                            (brow[:, 2, :], b3), (slot_no[:], iota[:, 0:CAP].to_broadcast((P, CAP))), (small, tri)):
                sp.dma_start(to, frm).then_inc(S["w_in"], 16)
            sp.wait_ge(S["consts_ready"], 1)
            sp.dma_start(bias3[:], bparts[:]).then_inc(S["b_in"], 16)
            sp.wait_ge(S["halo_ready"], 1)
            sp.dma_start(srt_d[0:1, :], halo[:, 0:2]).then_inc(S["halo_out"], 16)
            sp.dma_start(srt_d[EP + 1:EP + 2, :], halo[:, 2:4]).then_inc(S["halo_out"], 16)

            sp.wait_ge(S["buckets_ready"], 1)
            sp.dma_start(buckets_d, bucket).then_inc(S["bucket_out"], 16)
            sp.wait_ge(S["flag_ready"], 1)
            unfit = sp.value_load(flag[0:1, 0:1], min_val=0, max_val=1)
            with sp.If(unfit):
                sp.dma_start(jrow, iota[:, 0:CH].to_broadcast((P, CH))).then_inc(S["chunk_in"], 16)
                with sp.Fori(0, EP // CH) as c:
                    sp.wait_ge(S["chunk_used"], c + 1)
                    sp.dma_start(kb_i, key_row[:, bass.ds(c * CH, CH)].to_broadcast((P, CH))).then_inc(S["chunk_in"], 16)
                sp.wait_ge(S["sorted_done"], 1)
            with sp.Else():
                sp.wait_ge(S["srt_ready"], 1)
                sp.dma_start(srt_d[1:EP + 1, :].rearrange("(p j) w -> p j w", p=P), srt).then_inc(S["srt_out"], 16)
                sp.wait_ge(S["srt_out"], 16)

            sp.wait_ge(S["halo_out"], 32)
            for to, first in ((srow, 1), (nrow, 2)):
                sp.dma_start(to[:, 0], srt_d[first:first + P * P, :].rearrange("(t p) w -> t p w", p=P)
                             ).then_inc(S["srt_in"], 16)
                sp.dma_start(to[0:T - P, 1], srt_d[first + P * P:first + EP, :].rearrange("(t p) w -> t p w", p=P)
                             ).then_inc(S["srt_in"], 16)
            sp.dma_start(key_g[:], bass.AP(tensor=srt_d.tensor, offset=0, ap=[[2 * GE, G], [1, 2 * (GE + 1)]])
                         ).then_inc(S["srt_in"], 16)
            sp.wait_ge(S["far_ready"], 1)
            sp.dma_start(far_d, far_g[:]).then_inc(S["far_out"], 16)

            def rows_of(t, d):
                if t.fixed and t.i(d) == NB - 1:
                    return slice(LASTROW, N)
                return bass.ds(t.i(d) * BN, BN)

            def load_block(t, d):
                if not t.live(d, NB):
                    return
                if not t.fixed or t.i(d) >= RING:
                    wait(sp, S["norm_done"], t, d + RING)
                sp.dma_start(xin[:, t.slot(d)], xw[rows_of(t, d), :].rearrange("(p r) h -> p r h", p=P)
                             ).then_inc(x_in[t.slot(d)], 16)

            def load_ef(t, d):
                if not t.live(d, G):
                    return
                wait(sp, S["mm1_done"], t, d + RING)
                sp.dma_start(ef[:, t.slot(d), :], ef_t[:, bass.ds(t.i(d) * GE, GE)]).then_inc(ef_in[t.slot(d)], 16)

            for j in range(AHEAD):
                load_block(Turn(0, j), 0)
                load_ef(Turn(0, j), 0)

            def body(t):
                load_block(t, -AHEAD)
                load_ef(t, -AHEAD)
                if t.live(2):
                    wait(sp, S["rec_s"], t, 2)
                    wait(sp, S["rec_msg"], t, 2)
                    sp.dma_start(rec_d[bass.ds(t.i(2) * GE, GE), :].rearrange("(q p) w -> p q w", p=P),
                                 rec[:, t.slot(2)]).then_inc(rec_out[t.slot(2)], 16)
                if t.live(3, NB):
                    wait(sp, S["norm_done"], t, 3)
                    if t.fixed and t.i(3) == NB - 1:
                        wait_round(sp, stored, t, 4, 16)
                    sp.dma_start(out[rows_of(t, 3), :].rearrange("(p r) h -> p r h", p=P), xout[:, t.slot(3, XO)]
                                 ).then_inc(stored[t.slot(3, XO)], 16)

            rounds(sp, body)
            for r in range(XO):
                sp.wait_ge(stored[r], 16 * len(range(r, NB, XO)))
            sp.sem_inc(S["dense_written"], 1)
            for r in range(RING):
                sp.wait_ge(rec_out[r], 16 * len(range(r, G, RING)))
            sp.sem_inc(S["rec_written"], 1)

            sp.wait_ge(S["far_out"], 16)

            def load_far(t, d):
                if not t.live(d, G):
                    return
                wait(sp, S["m_ready"], t, d + RING)
                wait(sp, S["dt_ready"], t, d + RING)
                sp.dma_start(far[:, t.slot(d), :], far_d[bass.ds(t.i(d), 1), :].to_broadcast((P, GE))
                             ).then_inc(far_in[t.slot(d)], 16)

            for j in range(AHEAD):
                load_far(Turn(0, j), 0)
            rounds(sp, lambda t: load_far(t, -AHEAD))

        @block.gpsimd
        def _(pool):
            def rows_in(to, index, sems, r):
                for q in range(TPG):
                    pool.indirect_dma_start(out=to(q), out_offset=None, in_=xw,
                                            in_offset=bass.IndirectOffsetOnAxis(ap=index(q), axis=0)).then_inc(sems[r], 16)

            def sort_moves():
                pool.wait_ge(S["bucket_out"], 16)
                pool.wait_ge(S["pick_ready"], 1)
                for n in range(NEAR):
                    pool.indirect_dma_start(out=pick[:, n, :], out_offset=None, in_=buckets_d,
                                            in_offset=bass.IndirectOffsetOnAxis(ap=picki[:, n:n + 1], axis=1)
                                            ).then_inc(S["picked"], 16)
                pool.wait_ge(S["flag_ready"], 1)
                unfit = pool.value_load(flag[0:1, 0:1], min_val=0, max_val=1)
                with pool.If(unfit):
                    pool.sem_inc(S["rank_free"], 1)
                    with pool.Fori(0, G) as g:
                        pool.wait_ge(S["rank_staged"], g + 1)
                        pool.sem_inc(S["pool_turn"], 1)
                        for q in range(TPG):
                            pool.indirect_dma_start(
                                out=srt_d, out_offset=bass.IndirectOffsetOnAxis(ap=sistage[:, q:q + 1], axis=0),
                                in_=sstage[:, q, :], in_offset=None, bounds_check=EP, oob_is_err=False
                            ).then_inc(S["rank_scattered"], 16)
                        pool.wait_ge(S["rank_scattered"], (g + 1) * (16 * TPG))
                        pool.sem_inc(S["rank_free"], 1)
                    pool.sem_inc(S["sorted_done"], 1)

            def gather(t, d):
                if not t.live(d, G):
                    return
                r = t.slot(d)
                wait(pool, S["gidx_ready"], t, d)
                wait(pool, S["T_ready"], t, d + RING)
                wait(pool, S["rec_msg"], t, d + RING)
                pool.sem_inc(S["pool_turn"], 1)
                rows_in(lambda q: hs[:, r, q, :], lambda q: gidx[:, r, TPG + q:TPG + q + 1], hs_in, r)
                wait_round(pool, rec_out, t, d + RING, 16)
                pool.sem_inc(S["pool_turn"], 1)
                rows_in(lambda q: rec[:, r, q, H:RW], lambda q: gidx[:, r, q:q + 1], hk_in, r)

            for j in range(AHEAD):
                gather(Turn(0, j), 0)
            sort_moves()
            rounds(pool, lambda t: gather(t, -AHEAD))

            def gather_back(t, d):
                if not t.live(d, G):
                    return
                r = t.slot(d)
                wait(pool, S["ridx_ready"], t, d)
                wait(pool, S["y_done"], t, d + RING, per=TPG)
                pool.sem_inc(S["pool_turn"], 1)
                for q in range(TPG):
                    pool.indirect_dma_start(
                        out=back[:, r, q, :], out_offset=None, in_=rec_d,
                        in_offset=bass.IndirectOffsetOnAxis(ap=ridx[:, r, q:q + 1], axis=0)).then_inc(back_in[r], 16)

            def scatter(t, d):
                if not t.live(d, G):
                    return
                r = t.slot(d)
                wait(pool, S["res_ready"], t, d)
                wait(pool, S["sidx_ready"], t, d)
                pool.sem_inc(S["pool_turn"], 1)
                for q in range(TPG):
                    pool.indirect_dma_start(
                        out=out, out_offset=bass.IndirectOffsetOnAxis(ap=sidx[:, r, q:q + 1], axis=0),
                        in_=res[:, r, q, :], in_offset=None, bounds_check=N - 1, oob_is_err=False
                    ).then_inc(scattered[r], 16)

            pool.wait_ge(S["rec_written"], 1)
            for j in range(AHEAD):
                gather_back(Turn(0, j), 0)
            pool.wait_ge(S["dense_written"], 1)

            def body2(t):
                gather_back(t, -AHEAD)
                scatter(t, 3)

            rounds(pool, body2)
            for r in range(RING):
                pool.wait_ge(scattered[r], 16 * TPG * len(range(r, G, RING)))

        @block.scalar
        def _(act):
            def dense_norm(t, d, lo, hi):
                if not t.live(d, NB):
                    return
                if lo == 0:
                    wait(act, S["chain1"], t, d, per=STEPS)
                    wait_round(act, stored, t, d + XO, 16)
                    wait_round(act, x_in, t, d, 16)
                for j in range(lo, hi):
                    ins = nc.scalar.activation(xout[:, t.slot(d, XO), j, :], xin[:, t.slot(d), j, 0:H], ACT.Identity,
                                               bias=rs[:, t.slot(d, 2), 1, j:j + 1], scale=rs[:, t.slot(d, 2), 0, j:j + 1])
                if hi == BR:
                    ins.then_inc(S["norm_done"], 1)

            def body(t):
                if t.live(1):
                    wait(act, S["mm2_done"], t, 1)
                    wait(act, S["x2_ready"], t, 2)
                    nc.scalar.activation(th2[:], p_2[:], ACT.Tanh, scale=0.5).then_inc(S["th2_ready"], 1)
                if t.live(0):
                    wait(act, S["T_ready"], t, 0)
                    wait(act, S["mm1_done"], t, 1)
                    wait(act, S["proj_ready"], t, 1)
                    nc.scalar.activation(hT[:], p_hT[:], ACT.Copy).then_inc(S["hT_ready"], 1)
                dense_norm(t, 2, 0, 4)
                if t.live(0):
                    wait(act, S["mm1_done"], t, 0)
                    wait(act, S["x1_ready"], t, 1)
                    nc.scalar.activation(th1[:], p_1[:], ACT.Tanh, scale=0.5).then_inc(S["th1_ready"], 1)
                dense_norm(t, 2, 4, BR)

            rounds(act, body)

            def body2(t):
                if t.live(0):
                    wait(act, S["dt_ready"], t, 0)
                    wait(act, S["z_ready"], t, 2)
                    nc.scalar.activation(pa[:, t.slot(0, 2)], p_dt[:], ACT.Exp).then_inc(S["pa_ready"], 1)

            rounds(act, body2)

        @block.tensor
        def _(pe):
            pe.wait_ge(S["w_in"], 192)
            pe.wait_ge(S["consts_ready"], 2)
            p_cnt = p_dt[:, 0, :].rearrange("p (q b) -> p q b", q=TPG)
            p_place = p_w[:, 0:CAP]

            def sort_body(t):
                if t.live(1):
                    wait(pe, S["pos_ready"], t, 1)
                    for q in range(TPG):
                        for o in range(q, TPG):
                            pe.matmul(p_cnt[:, q, :], after16[:] if o == q else all16[:], hot16[:, t.slot(1, 2), o, :],
                                      start=False, stop=True, skip_group_check=True)
                if t.live(0):
                    wait(pe, S["hot_ready"], t, 0)
                    for q in range(TPG):
                        for o in range(q + 1):
                            first = t.fixed and t.i() == 0 and q == 0
                            ins = pe.matmul(p_cnt[:, q, :], before16[:] if o == q else all16[:], hot16[:, t.slot(0, 2), o, :],
                                            start=first, stop=True, skip_group_check=True)
                    ins.then_inc(S["cnt_ready"], 1)
                if t.live(1):
                    wait(pe, S["placed_ready"], t, 1)
                    for q in range(TPG):
                        first = t.fixed and t.i(1) == 0 and q == 0
                        ins = pe.matmul(p_place, hot[:, t.slot(1, 2), q, :], placed[:, q, :], start=first, stop=True,
                                        skip_group_check=True)
                    ins.then_inc(S["place_done"], 1)

            rounds(pe, sort_body)
            pe.wait_ge(S["count_row"], 1)
            pe.matmul(p_1[:, 0:1], counts, ident[:, 0:1], start=True, stop=True).then_inc(S["count_col"], 1)
            pe.wait_ge(S["viol"], 1)
            pe.matmul(p_2[:, 0:1], ones[:], cols[:, 0:1], start=True, stop=True).then_inc(S["viol_sum"], 1)

            pe.wait_ge(S["srt_in"], 80)
            for n, (row, w, to) in enumerate(((srow, 0, p_hT[:, 0, :]), (nrow, 0, p_hT[:, 1, :]), (srow, 1, p_1[:]))):
                pe.transpose(to[:, 0:P], row[:, 0, :, w], ident[:])
                pe.transpose(to[:, P:T], row[0:T - P, 1, :, w], ident[0:T - P, 0:T - P]).then_inc(S["srt_T"], 1)
            pe.wait_ge(S["b_in"], 16)
            pe.wait_ge(S["tables_ready"], 1)

            def body(t):
                if t.live(1):
                    wait(pe, S["x1_ready"], t, 1)
                    wait(pe, S["x2_ready"], t, 2)
                    pe.matmul(p_2[:], w2h[:], x1[:], start=True, stop=False)
                    pe.matmul(p_2[:], bias3[:, 1, :], ones16[:], start=False, stop=True).then_inc(S["mm2_done"], 1)
                if t.live(0):
                    wait(pe, S["hT_ready"], t, 1)
                    wait_round(pe, hs_in, t, 0, 64)
                    for q in range(TPG):
                        pe.transpose(p_hT[:, 1, q * P:(q + 1) * P], hs[:, t.slot(), q, 0:H], ident[:])
                    wait_round(pe, hk_in, t, 0, 64)
                    for q in range(TPG):
                        ins = pe.transpose(p_hT[:, 0, q * P:(q + 1) * P], rec[:, t.slot(), q, H:2 * H], ident[:])
                    ins.then_inc(S["T_ready"], 1)
                if t.live(1):
                    wait(pe, S["x2_ready"], t, 1)
                    wait(pe, S["rec_s"], t, 2)
                    for q in range(TPG):
                        pe.matmul(p_w[:, q:q + 1], x2[:, q * P:(q + 1) * P], w3h[:], start=True, stop=False)
                        ins = pe.matmul(p_w[:, q:q + 1], ones16[:, 0:P], bias3[:, 2, 0:1], start=False, stop=True)
                    ins.then_inc(S["s_ready"], 1)
                if t.live(0):
                    wait(pe, S["hT_ready"], t, 0)
                    wait(pe, S["x1_ready"], t, 1)
                    wait_round(pe, ef_in, t, 0, 16)
                    pe.matmul(p_1[:], w1a[:], hT[:, 0, :], start=True, stop=False)
                    pe.matmul(p_1[:], w1b[:], hT[:, 1, :], start=False, stop=False)
                    pe.matmul(p_1[:], w1c[:], ef[:, t.slot(), :], start=False, stop=False)
                    pe.matmul(p_1[:], bias3[:, 0, :], ones16[:], start=False, stop=True).then_inc(S["mm1_done"], 1)
                    wait(pe, S["rec_msg"], t, 1)
                    for q in range(TPG):
                        ins = pe.matmul(p_m[:, q, :], hT[:, 1, q * P:(q + 1) * P], wvs[:], start=True, stop=True)
                    ins.then_inc(S["proj_ready"], 1)

            rounds(pe, body)

            def body2(t):
                if t.live(1):
                    wait_round(pe, back_in, t, 1, 64)
                    wait(pe, S["y_done"], t, 2, per=TPG)
                    for q in range(TPG):
                        ins = pe.transpose(p_w[:, q * P:(q + 1) * P], back[:, t.slot(1), q, 0:H], ident[:])
                    ins.then_inc(S["mT_ready"], 1)
                if t.live(0):
                    wait_round(pe, back_in, t, 0, 64)
                    wait(pe, S["pa_ready"], t, 1)
                    for q in range(TPG):
                        ins = pe.matmul(p_dt[:, 0, q * P:(q + 1) * P],
                                        back[:, t.slot(), q, RW - 1:RW].to_broadcast((P, P)), ident[:],
                                        start=(q == 0), stop=True, skip_group_check=True)
                    ins.then_inc(S["sb_ready"], 1)
                if t.live(1):
                    wait(pe, S["z_ready"], t, 1)
                    for q in range(TPG):
                        pe.matmul(p_2[:, q:q + 1], den[0:1, t.slot(1, 2), q * P:(q + 1) * P], ones[0:1, 0:1],
                                  start=True, stop=True)
                    for q in range(TPG):
                        ins = pe.transpose(p_m[:, q, :], z[:, t.slot(1, 2), q * P:(q + 1) * P], ident[:])
                    ins.then_inc(S["agg_ready"], 1)
                if t.live(0):
                    wait(pe, S["m_ready"], t, 0)
                    wait_round(pe, far_in, t, 0, 16)
                    m = mx[:, t.slot(0, 2), :]
                    pe.matmul(p_dt[:, 0, :], nident[:], m[:, 1:GE + 1], start=False, stop=True, skip_group_check=True)
                    pe.matmul(p_dt[:, 1, :], ident16[:], far[:, t.slot(), :], start=True, stop=False)
                    pe.matmul(p_dt[:, 1, :], ident[:], m[:, 0:GE], start=False, stop=False)
                    pe.matmul(p_dt[:, 1, :], nident[:], m[:, 1:GE + 1], start=False, stop=True).then_inc(S["dt_ready"], 1)

            rounds(pe, body2)

        @block.vector
        def _(dve):
            vec = nc.vector
            count = [0]

            def link(ins, s="setup"):
                count[0] += 1
                ins.then_inc(S[s], 1)
                dve.wait_ge(S[s], count[0])

            dve.wait_ge(S["t_in"], 48)
            vec.tensor_scalar(gidx_t[:, :, 0:TPG], rcv_t[:].rearrange("p (g q) -> p g q", q=TPG), float(N - 1), None, ALU.min)
            vec.tensor_copy(gidx_t[:, :, TPG:2 * TPG], snd_t[:].rearrange("p (g q) -> p g q", q=TPG))
            vec.tensor_copy(keyid[:, :, 0], rcv_t[:])
            vec.tensor_copy(keyid[:, :, 1], idrel[:])
            vec.memset(rank[:], 1.0)
            vec.memset(cnt_lt[:], 0.0)
            vec.memset(cnt_eq[:], 0.0)
            vec.memset(halo[:, 0:2], -1.0)
            link(vec.memset(halo[:, 2:4], float(N + 1)))
            vec.memset(ones[:], 1.0).then_inc(S["halo_ready"], 1)
            vec.tensor_scalar(ranki[:], rcv_t[:], 10, None, ALU.logical_shift_right)
            link(vec.tensor_scalar(q_i[:], rcv_t[:], BUCKET - 1, None, ALU.bitwise_and))
            vec.tensor_copy(bno[:], ranki[:])
            link(vec.tensor_scalar(comp[:], q_i[:], -float(BUCKET // 2), float(EP), ALU.add, ALU.mult))
            link(vec.tensor_tensor(comp[:], comp[:], idrel[:], ALU.add))
            vec.memset(ones16[:], 1.0)
            dve.wait_ge(S["w_in"], 192)
            vec.tensor_scalar(nident[:], ident[:], -1.0, None, ALU.mult)
            vec.tensor_copy(ident16[:], ident[:])
            vec.tensor_scalar(w2h[:], w2s[:], 0.5, None, ALU.mult)
            vec.tensor_scalar(w3h[:], w3s[:], 0.5, None, ALU.mult)
            link(vec.tensor_copy(bparts[:, 0], brow[:]))
            link(vec.tensor_tensor(brest[:, 0], brow[:], bparts[:, 0], ALU.subtract))
            link(vec.tensor_copy(bparts[:, 1], brest[:, 0]))
            link(vec.tensor_tensor(brest[:, 1], brest[:, 0], bparts[:, 1], ALU.subtract))
            link(vec.tensor_copy(bparts[:, 2], brest[:, 1]))
            link(vec.memset(cw[:], 1.0))
            link(vec.memset(cols[:], 0.0))
            link(vec.memset(cw[:, 0, 0:1], 1.0))
            vec.memset(cw[:, 0, 0:1], 1.0).then_inc(S["consts_ready"], 2)

            def copy_gidx(t, d):
                if t.live(d, G):
                    wait_round(dve, hk_in, t, d + RING, 64)
                    wait_round(dve, hs_in, t, d + RING, 64)
                    g = t.i(d)
                    at = gidx_t[:, g, :] if t.fixed else gidx_t[:, bass.ds(g, 1), :].rearrange("p a q -> p (a q)")
                    vec.tensor_copy(gidx[:, t.slot(d), :], at).then_inc(S["gidx_ready"], 1)

            for j in range(AHEAD):
                copy_gidx(Turn(0, j), 0)

            vec.memset(all16[:], 1.0)
            vec.tensor_copy(before16[:], small)
            vec.tensor_scalar(after16[:], small, -1.0, 1.0, ALU.mult, ALU.add)
            vec.memset(bucket, BIG)

            def sort_body(t):
                if t.live(0):
                    wait(dve, S["place_done"], t, 2)
                    for q in range(TPG):
                        ins = vec.tensor_scalar(hot[:, t.slot(0, 2), q, :], slot_no[:, 0:P],
                                                bno[:, bass.ds(t.i() * TPG + q, 1)], None, ALU.is_equal)
                    ins.then_inc(S["sdve"], 1)
                if t.live(1):
                    wait(dve, S["cnt_ready"], t, 1)
                    wait(dve, S["placed_ready"], t, 2)
                    for q in range(TPG):
                        ins = vec.tensor_tensor_reduce(junk16[:, q, :], p_dt[:, 0, q * P:(q + 1) * P], hot[:, t.slot(1, 2), q, :],
                                                       1.0, 0.0, ALU.mult, ALU.add, pos[:, t.slot(1, 2), q:q + 1])
                    ins.then_inc(S["pos_ready"], 1)
                if t.live(0):
                    wait(dve, S["sdve"], t, 0)
                    vec.tensor_copy(hot16[:, t.slot(0, 2)], hot[:, t.slot(0, 2)]).then_inc(S["hot_ready"], 1)
                if t.live(1):
                    wait(dve, S["pos_ready"], t, 1)
                    wait(dve, S["place_done"], t, 2)
                    for q in range(TPG):
                        ins = vec.tensor_scalar(placed[:, q, :], slot_no[:], pos[:, t.slot(1, 2), q:q + 1],
                                                comp[:, bass.ds(t.i(1) * TPG + q, 1)], ALU.is_equal, ALU.mult)
                    ins.then_inc(S["placed_ready"], 1)

            rounds(dve, sort_body)
            dve.wait_ge(S["place_done"], G)
            link(vec.tensor_copy(counts, p_dt[:, 0, 0:P]))
            vec.tensor_copy(cols[:, 15:16], cols[:, 14:15]).then_inc(S["count_row"], 1)
            sc = {n: cols[:, m:m + 1] for m, n in enumerate(
                ("viol", "start", "end", "b0", "b1", "most", "unfit", "bk", "base", "off"))}
            link(vec.tensor_tensor_scan(incl, ones[:], counts, 0.0, ALU.mult, ALU.add))
            link(vec.tensor_scalar(sc["start"], idrel[:, 0:1], float(ROWLEN), None, ALU.mult))
            link(vec.tensor_scalar(sc["end"], sc["start"], float(ROWLEN - 1), None, ALU.add))
            link(vec.tensor_scalar(small, incl, sc["start"], None, ALU.is_le))
            link(vec.tensor_reduce(sc["b0"], small, mybir.AxisListType.X, ALU.add))
            link(vec.tensor_scalar(small, incl, sc["end"], None, ALU.is_le))
            link(vec.tensor_reduce(sc["b1"], small, mybir.AxisListType.X, ALU.add))
            link(vec.tensor_reduce(sc["most"], counts, mybir.AxisListType.X, ALU.max))
            link(vec.tensor_tensor(sc["b1"], sc["b1"], sc["b0"], ALU.subtract))
            link(vec.tensor_scalar(sc["unfit"], sc["b1"], float(NEAR - 1), None, ALU.is_gt))
            link(vec.tensor_scalar(sc["most"], sc["most"], float(CAP), None, ALU.is_gt))
            link(vec.tensor_tensor(sc["viol"], sc["most"], sc["unfit"], ALU.add))
            vec.tensor_copy(cols[:, 15:16], cols[:, 14:15]).then_inc(S["viol"], 1)
            for n in range(NEAR):
                link(vec.tensor_scalar(sc["bk"], sc["b0"], float(n), None, ALU.add))
                link(vec.scalar_tensor_tensor(out=small, in0=slot_no[:, 0:P], scalar=sc["bk"], in1=counts, op0=ALU.is_lt,
                                              op1=ALU.mult))
                link(vec.tensor_reduce(sc["base"], small, mybir.AxisListType.X, ALU.add))
                link(vec.tensor_tensor(sc["off"], sc["start"], sc["base"], ALU.subtract))
                link(vec.tensor_scalar(sc["off"], sc["off"], -float(ROWLEN + 4), float(PAD), ALU.max, ALU.add))
                link(vec.tensor_scalar(sc["off"], sc["off"], float(CAP + PAD), None, ALU.min))
                link(vec.scalar_tensor_tensor(out=sc["off"], in0=sc["bk"], scalar=float(PITCH), in1=sc["off"], op0=ALU.mult,
                                              op1=ALU.add))
                link(vec.tensor_copy(picki[:, n:n + 1], sc["off"]))
            vec.tensor_copy(cols[:, 15:16], cols[:, 14:15]).then_inc(S["pick_ready"], 1)
            dve.wait_ge(S["viol_sum"], 1)
            link(vec.tensor_scalar(flag[:], p_2[:, 0:1], 0.5, None, ALU.is_gt))
            vec.tensor_copy(cols[:, 15:16], cols[:, 14:15]).then_inc(S["flag_ready"], 1)

            dve.wait_ge(S["count_col"], 1)
            link(vec.tensor_scalar(other[:, 0:CAP], slot_no[:], p_1[:, 0:1], BIG, ALU.is_ge, ALU.mult))
            row = bucket[:, PAD:PAD + SORTW]
            link(vec.tensor_tensor(row[:, 0:CAP], p_w[:, 0:CAP], other[:, 0:CAP], ALU.add))
            frm, to = row, other
            k = 2
            while k <= SORTW:
                j = k // 2
                while j:
                    def halves(x, down):
                        if k == SORTW:
                            w = x.rearrange("p (c two j) -> p c two j", two=2, j=j)
                            return w[:, :, 0, :], w[:, :, 1, :]
                        w = x.rearrange("p (m d k) -> p m d k", d=2, k=k)[:, :, down, :]
                        w = w.rearrange("p m (c two j) -> p m c two j", two=2, j=j)
                        return w[:, :, :, 0, :], w[:, :, :, 1, :]
                    for down in range(1 if k == SORTW else 2):
                        lo, hi = halves(frm, down)
                        tlo, thi = halves(to, down)
                        vec.tensor_tensor(tlo, lo, hi, ALU.max if down else ALU.min)
                        ins = vec.tensor_tensor(thi, lo, hi, ALU.min if down else ALU.max)
                    link(ins)
                    frm, to = to, frm
                    j //= 2
                k *= 2
            if frm is not row:
                link(vec.tensor_copy(row, frm))
            vec.tensor_copy(cols[:, 15:16], cols[:, 14:15]).then_inc(S["buckets_ready"], 1)

            unfit = dve.value_load(flag[0:1, 0:1], min_val=0, max_val=1)
            with dve.If(unfit):
                vec.memset(junk, 0.0).then_inc(S["chunk_used"], 1)
                per = 3 + 3 * T
                with dve.Fori(0, EP // CH) as c:
                    dve.wait_ge(S["chunk_in"], c * 16 + 32)
                    vec.tensor_copy(kb, kb_i).then_inc(S["slow"], 1)
                    dve.wait_ge(S["slow"], c * per + 1)
                    vec.memset(cw[:, 0, 1:2], 1.0)
                    with dve.Fori(0, T) as t:
                        base = c * per + t * 3 + 1
                        key = keyid[:, bass.ds(t, 1), 0]
                        vec.tensor_scalar(junk, kb, key, 0.0, ALU.is_lt, ALU.add, accum_out=cnt_lt[:, bass.ds(t, 1)])
                        vec.tensor_scalar(jm, jrow, idrel[:, bass.ds(t, 1)], None, ALU.is_lt).then_inc(S["slow"], 1)
                        dve.wait_ge(S["slow"], base + 1)
                        vec.scalar_tensor_tensor(out=junk, in0=kb, scalar=key, in1=jm, op0=ALU.is_equal, op1=ALU.mult
                                                 ).then_inc(S["slow"], 1)
                        dve.wait_ge(S["slow"], base + 2)
                        vec.tensor_reduce(cnt_eq[:, bass.ds(t, 1)], junk, mybir.AxisListType.X, ALU.add).then_inc(S["slow"], 1)
                        dve.wait_ge(S["slow"], base + 3)
                    vec.tensor_tensor(rank[:], rank[:], cnt_lt[:], ALU.add).then_inc(S["slow"], 1)
                    dve.wait_ge(S["slow"], c * per + (3 * T + 2))
                    vec.tensor_scalar(idrel[:], idrel[:], -float(CH), None, ALU.add)
                    vec.tensor_tensor(rank[:], rank[:], cnt_eq[:], ALU.add).then_inc(S["slow"], 1)
                    dve.wait_ge(S["slow"], c * per + (3 * T + 3))
                    vec.memset(cw[:, 0, 0:1], 1.0).then_inc(S["chunk_used"], 1)
                vec.tensor_copy(ranki[:], rank[:]).then_inc(S["slow"], 1)
                dve.wait_ge(S["slow"], (EP // CH) * (3 + 3 * T) + 1)
                with dve.Fori(0, G) as g:
                    with_g = bass.ds(g * TPG, TPG)
                    dve.wait_ge(S["rank_free"], g + 1)
                    vec.tensor_copy(sistage[:], ranki[:, with_g])
                    vec.tensor_copy(sstage[:], keyid[:, with_g, :]).then_inc(S["rank_staged"], 1)


            dve.wait_ge(S["picked"], 16 * NEAR)
            val, bq, qf, idd, t1 = srt[:, :, 0], srt[:, :, 1], placed[:, 0, 0:ROWLEN], placed[:, 1, 0:ROWLEN], placed[:, 2, 0:ROWLEN]
            link(vec.tensor_tensor(val, pick[:, 0, :], pick[:, 1, :], ALU.min))
            for n in range(2, NEAR):
                link(vec.tensor_tensor(val, val, pick[:, n, :], ALU.min))
            for n in range(1, NEAR):
                link(vec.tensor_scalar(pick[:, n, :], pick[:, n, :], BIG / 2, float(n), ALU.is_lt, ALU.mult))
            link(vec.tensor_tensor(bq, pick[:, 1, :], pick[:, 2, :], ALU.add))
            link(vec.tensor_scalar(bq, bq, sc["b0"], float(BUCKET), ALU.add, ALU.mult))
            link(vec.tensor_scalar(q_i[:], val, 1.0 / EP, None, ALU.mult))
            link(vec.tensor_copy(qf, q_i[:]))
            link(vec.scalar_tensor_tensor(out=idd, in0=qf, scalar=-float(EP), in1=val, op0=ALU.mult, op1=ALU.add))
            link(vec.tensor_scalar(t1, idd, 0.0, None, ALU.is_lt))
            link(vec.tensor_tensor(qf, qf, t1, ALU.subtract))
            link(vec.scalar_tensor_tensor(out=idd, in0=t1, scalar=float(EP), in1=idd, op0=ALU.mult, op1=ALU.add))
            link(vec.tensor_scalar(t1, idd, float(EP), None, ALU.is_ge))
            link(vec.tensor_tensor(qf, qf, t1, ALU.add))
            link(vec.scalar_tensor_tensor(out=t1, in0=t1, scalar=-float(EP), in1=idd, op0=ALU.mult, op1=ALU.add))
            link(vec.tensor_scalar(qf, qf, float(BUCKET // 2), None, ALU.add))
            link(vec.tensor_tensor(qf, bq, qf, ALU.add))
            link(vec.tensor_copy(srt[:, :, 0], qf))
            link(vec.tensor_copy(srt[:, :, 1], t1))
            vec.tensor_copy(cols[:, 15:16], cols[:, 14:15]).then_inc(S["srt_ready"], 1)

            dve.wait_ge(S["srt_in"], 80)
            link(vec.tensor_tensor(far_g[:], key_g[:, 1:GE + 1, 0], key_g[:, 0:GE, 0], ALU.not_equal))
            link(vec.tensor_scalar(far_g[:], far_g[:], FAR, None, ALU.mult))
            vec.memset(cw[:, 0, 0:1], 1.0).then_inc(S["far_ready"], 1)
            dve.wait_ge(S["srt_T"], 3)
            vec.tensor_copy(id_s[:], p_1[:, 0:T])
            link(vec.tensor_copy(key_s[:], p_hT[:, 0, 0:T]))
            link(vec.tensor_tensor(next_s[:], key_s[:], p_hT[:, 1, 0:T], ALU.is_equal))
            link(vec.scalar_tensor_tensor(out=sidx_t[:], in0=next_s[:], scalar=SKIP, in1=key_s[:], op0=ALU.mult, op1=ALU.add))

            vec.memset(mx[:, 0, 0:1], 0.0)
            vec.memset(den[:, 1, GE - 1:GE], 0.0)
            vec.memset(z[:, 1, GE - 1:GE], 0.0)
            vec.memset(cw[:, 0, 0:1], 1.0).then_inc(S["tables_ready"], 1)

            def chain(t, d, n, s, o, step_sem, stats_sem, gate):
                sm, dl, q, va, a, b = (cw[:, m, 0:n] for m in range(6))
                r, bi = o[:, 0, 0:n], o[:, 1, 0:n]
                ri, vi, ai = r.bitcast(I32), va.bitcast(I32), a.bitcast(I32)
                s = s[:, 0:n, :]

                def step(ins):
                    ins.then_inc(step_sem, 1)

                def after(m):
                    wait(dve, step_sem, t, d, per=STEPS, off=m - STEPS)

                wait(dve, stats_sem, t, d)
                step(vec.tensor_tensor(dl, s[:, :, 1], s[:, :, 4], ALU.subtract)); yield
                step(vec.tensor_tensor(sm, s[:, :, 1], s[:, :, 4], ALU.add)); yield
                step(vec.tensor_tensor(q, s[:, :, 2], s[:, :, 5], ALU.add)); yield
                after(1)
                step(vec.tensor_tensor(a, dl, dl, ALU.mult)); yield
                after(4)
                step(vec.scalar_tensor_tensor(out=b, in0=a, scalar=32.0, in1=q, op0=ALU.mult, op1=ALU.add)); yield
                after(5)
                step(vec.tensor_scalar(va, b, 1.0 / H, EPS_LN / 4, ALU.mult, ALU.add)); yield
                after(6)
                step(vec.tensor_scalar(ai, vi, 1, None, ALU.logical_shift_right)); yield
                after(7)
                gate()
                step(vec.tensor_scalar(ri, ai, -1.0, MAGIC, ALU.mult, ALU.add)); yield
                for m in range(3):
                    after(8 + 3 * m)
                    step(vec.scalar_tensor_tensor(out=a, in0=r, scalar=-0.5, in1=r, op0=ALU.mult, op1=ALU.mult)); yield
                    after(9 + 3 * m)
                    step(vec.tensor_tensor(b, a, va, ALU.mult)); yield
                    after(10 + 3 * m)
                    step(vec.scalar_tensor_tensor(out=r, in0=b, scalar=1.5, in1=r, op0=ALU.add, op1=ALU.mult)); yield
                after(17)
                step(vec.scalar_tensor_tensor(out=bi, in0=sm, scalar=-0.5, in1=r, op0=ALU.mult, op1=ALU.mult)); yield
                after(18)

            def body(t):
                def gate():
                    if t.live(3, NB):
                        wait(dve, S["norm_done"], t, 3)

                steps = iter(())
                if t.live(1, NB):
                    steps = chain(t, 1, BR, st[:, t.slot(1, 2)], rs[:, t.slot(1, 2)], S["chain1"], S["dense_stats"], gate)

                def more(n=1):
                    for _ in range(n):
                        next(steps, None)

                def stats(lo, hi):
                    if not t.live(0, NB):
                        return
                    if lo == 0:
                        wait_round(dve, x_in, t, 0, 16)
                    for j in range(lo, hi):
                        ins = vec.bn_stats(st[:, t.slot(0, 2), j, :], xin[:, t.slot(), j, 0:H])
                        if j == BR - 1:
                            ins.then_inc(S["dense_stats"], 1)
                        more()

                copy_gidx(t, -AHEAD)
                stats(0, 4)
                if t.live(1):
                    wait(dve, S["th2_ready"], t, 1)
                    wait(dve, S["s_ready"], t, 2)
                    vec.scalar_tensor_tensor(out=x2[:], in0=th2[:], scalar=1.0, in1=p_2[:], op0=ALU.add, op1=ALU.mult
                                             ).then_inc(S["x2_ready"], 1)
                more()
                stats(4, 10)
                if t.live(0):
                    wait(dve, S["th1_ready"], t, 0)
                    wait(dve, S["mm2_done"], t, 1)
                    vec.scalar_tensor_tensor(out=x1[:], in0=th1[:], scalar=1.0, in1=p_1[:], op0=ALU.add, op1=ALU.mult
                                             ).then_inc(S["x1_ready"], 1)
                more()
                if t.live(1):
                    wait(dve, S["s_ready"], t, 1)
                    vec.tensor_copy(rec[:, t.slot(1), :, RW - 1], p_w[:, 0:TPG]).then_inc(S["rec_s"], 1)
                stats(10, BR)
                if t.live(0):
                    wait(dve, S["proj_ready"], t, 0)
                    wait_round(dve, rec_out, t, RING, 16)
                    w = hs[:, t.slot(), :, H:H + 1].to_broadcast((P, TPG, H))
                    vec.tensor_tensor(rec[:, t.slot(), :, 0:H], p_m[:], w, ALU.mult).then_inc(S["rec_msg"], 1)
                more(99)

            rounds(dve, body)

            def copy_ridx(t, d):
                if t.live(d, G):
                    wait_round(dve, back_in, t, d + RING, 64)
                    vec.tensor_copy(ridx[:, t.slot(d), :], column(id_s, t.i(d), t.fixed)).then_inc(S["ridx_ready"], 1)

            for j in range(AHEAD):
                copy_ridx(Turn(0, j), 0)
            yb = [y0, y1]

            def body2(t):
                steps = iter(())
                if t.live(2):
                    steps = chain(t, 2, TPG, st[:, t.slot(2, 2)], rs[:, t.slot(2, 2)], S["chain2"], S["edge_stats"],
                                  lambda: None)

                def more(n=1):
                    for _ in range(n):
                        next(steps, None)

                copy_ridx(t, -AHEAD)
                more()
                if t.live(1):
                    pp = pa[:, t.slot(1, 2)]
                    wait(dve, S["pa_ready"], t, 1)
                    wait(dve, S["agg_ready"], t, 3)
                    vec.tensor_tensor_scan(den[:, t.slot(1, 2), :], pp[:, 1, :], pp[:, 0, :],
                                           den[:, t.slot(2, 2), GE - 1:GE], ALU.mult, ALU.add)
                    more(2)
                    wait(dve, S["mT_ready"], t, 1)
                    vec.tensor_tensor(v[:], pp[:, 0, :], p_w[:], ALU.mult).then_inc(S["v_ready"], 1)
                    more(3)
                    wait(dve, S["v_ready"], t, 1)
                    vec.tensor_tensor_scan(z[:, t.slot(1, 2), :], pp[:, 1, :], v[:], z[:, t.slot(2, 2), GE - 1:GE],
                                           ALU.mult, ALU.add).then_inc(S["z_ready"], 1)
                    more(2)
                if t.live(0):
                    m = mx[:, t.slot(0, 2), :]
                    wait(dve, S["sb_ready"], t, 0)
                    wait(dve, S["dt_ready"], t, 2)
                    wait_round(dve, far_in, t, 0, 16)
                    if not (t.fixed and t.i(0) == 0):
                        vec.tensor_copy(m[:, 0:1], mx[:, t.slot(1, 2), GE:GE + 1])
                    vec.tensor_tensor_scan(m[:, 1:GE + 1], far[:, t.slot(), :], p_dt[:, 0, :],
                                           0.0 if t.fixed and t.i(0) == 0 else mx[:, t.slot(1, 2), GE:GE + 1],
                                           ALU.add, ALU.max).then_inc(S["m_ready"], 1)
                    more(4)
                if t.live(1):
                    wait(dve, S["agg_ready"], t, 1)
                    vec.tensor_scalar(rden[:, 0, :], p_2[:, 0:TPG], 2.0, 2 * EPS_DEN, ALU.mult, ALU.add
                                      ).then_inc(S["rden_ready"], 1)
                    more(1)
                    wait(dve, S["rden_ready"], t, 1, per=2, off=-1)
                    vec.reciprocal(rden[:, 1, :], rden[:, 0, :]).then_inc(S["rden_ready"], 1)
                    more(1)
                    wait(dve, S["rden_ready"], t, 1, per=2)
                    for q in range(TPG):
                        vec.scalar_tensor_tensor(out=yb[t.slot(1, 2)][:, q * H:(q + 1) * H], in0=p_m[:, q, :],
                                                 scalar=rden[:, 1, q:q + 1], in1=back[:, t.slot(1), q, H:2 * H],
                                                 op0=ALU.mult, op1=ALU.add).then_inc(S["y_done"], 1)
                        more(1)
                    for q in range(TPG):
                        wait(dve, S["y_done"], t, 1, per=TPG, off=q + 1 - TPG)
                        ins = vec.bn_stats(st[:, t.slot(1, 2), q, :], yb[t.slot(1, 2)][:, q * H:(q + 1) * H])
                        more(1)
                    ins.then_inc(S["edge_stats"], 1)
                more(99)
                if t.live(2):
                    wait_round(dve, scattered, t, 2 + RING, 64)
                    for q in range(TPG):
                        ins = vec.tensor_scalar(res[:, t.slot(2), q, :], yb[t.slot(2, 2)][:, q * H:(q + 1) * H],
                                                rs[:, t.slot(2, 2), 0, q:q + 1],
                                                rs[:, t.slot(2, 2), 1, q:q + 1], ALU.mult, ALU.add)
                    ins.then_inc(S["res_ready"], 1)
                    vec.tensor_copy(sidx[:, t.slot(2), :], column(sidx_t, t.i(2), t.fixed)).then_inc(S["sidx_ready"], 1)

            rounds(dve, body2)


def kernel(x, src, dst, edge_attr_3, edge_weight1, node_vec, L0_gnn_W1, L0_gnn_b1, L0_gnn_W2, L0_gnn_b2, L0_gnn_W3,
           L0_gnn_b3, L0_gnn_Wv):
    import numpy as np
    import concourse.bacc as bacc
    from concourse import mybir as mb
    from concourse.bass_utils import run_bass_kernel_spmd

    src = np.asarray(src)
    dst = np.asarray(dst)
    rcv = np.full(EP, N, src.dtype)
    rcv[:E] = src
    snd = np.zeros(EP, dst.dtype)
    snd[:E] = dst
    ef = np.zeros((4, EP), np.float32)
    ef[0:3, :E] = np.asarray(edge_attr_3).T
    ef[3, :E] = np.asarray(edge_weight1)[:, 0]

    def nat(a):
        return np.ascontiguousarray(a.reshape(G * TPG, P).T)

    arrays = {
        "xw": np.concatenate([np.asarray(x), np.asarray(node_vec)[:, None]], axis=1),
        "snd_nat": nat(snd),
        "rcv_nat": nat(rcv),
        "id_nat": nat(np.arange(EP, dtype=np.float32)),
        "key_row": rcv.reshape(1, EP),
        "iota": np.arange(CH, dtype=np.float32).reshape(1, CH),
        "tri": np.triu(np.ones((P, P), np.float32), 1),
        "ef_t": ef,
        "w1": np.asarray(L0_gnn_W1),
        "b1": np.asarray(L0_gnn_b1).reshape(1, H),
        "w2": np.asarray(L0_gnn_W2),
        "b2": np.asarray(L0_gnn_b2).reshape(1, H),
        "w3": np.asarray(L0_gnn_W3),
        "b3": np.ascontiguousarray(np.broadcast_to(np.asarray(L0_gnn_b3).reshape(1, 1), (1, H))),
        "wv": np.asarray(L0_gnn_Wv),
        "eye": np.eye(P, dtype=np.float32),
    }
    nc = bacc.Bacc("TRN2", target_bir_lowering=False, num_devices=1)
    feed, args = {}, []
    for name, a in arrays.items():
        a = np.ascontiguousarray(a)
        feed[f"in_{name}"] = a
        args.append(nc.dram_tensor(f"in_{name}", a.shape, mb.dt.from_np(a.dtype), kind="ExternalInput").ap())
    out = nc.dram_tensor("out_rows", (N, H), mb.dt.float32, kind="ExternalOutput").ap()
    gnn_kernel(nc, *args, out)
    r = run_bass_kernel_spmd(nc, [feed], core_ids=[0])
    return r.results[0]["out_rows"]
```

```python
from contextlib import ExitStack

import concourse.bass as bass
from concourse import mybir

F32 = mybir.dt.float32
BF16 = mybir.dt.bfloat16
I32 = mybir.dt.int32
ALU = mybir.AluOpType
ACT = mybir.ActivationFunctionType

P = 128
N = 100000
E = 25000
H = 128
TPG = 4
GE = TPG * P
G = -(-E // GE)
EP = G * GE
T = G * TPG
XW = H + 1
RW = H + XW
BR = 16
BN = P * BR
NB = -(-N // BN)
LASTROW = N - BN
RING = 4
ITERS = -(-(G + 3) // RING) * RING
ROUNDS = ITERS // RING
AHEAD = 2
ACT_ROWS = 13
XO = 2
BUCKET = 1024
CAP = 352
SORTW = 512
PITCH, PAD = 1024, 256
ROWLEN = EP // P
NEAR = 3
BIG = 1.0e9
CH = EP // 16
STEPS = 18
EPS_LN = 1e-5
EPS_DEN = 1e-12
FAR = -1.0e38
SKIP = float(1 << 20)
MAGIC = float(0x5F3759DF)
assert ITERS % RING == 0 and NB <= G and N <= P * BUCKET and (BUCKET // 2) * EP < 1 << 24


def gnn_kernel(nc, xw, snd_nat, rcv_nat, id_nat, key_row, iota, tri, ef_t, w1, b1, w2, b2, w3, b3, wv, eye, out):
    far_d = nc.dram_tensor("far_d", (G, GE), BF16).ap()
    rec_d = nc.dram_tensor("rec_d", (EP, RW), F32).ap()
    srt_d = nc.dram_tensor("srt_d", (EP + 2, 2), F32).ap()
    buckets_d = nc.dram_tensor("buckets_d", (P, PITCH), F32).ap()
    with ExitStack() as ctx:
        def sb(name, shape, dt=F32):
            return ctx.enter_context(nc.sbuf_tensor(name, shape, dt))

        def ps(name, shape):
            return ctx.enter_context(nc.psum_tensor(name, shape, F32))

        def sem(name):
            return ctx.enter_context(nc.semaphore(name))

        ident = sb("ident", [P, P])
        nident = sb("nident", [P, P])
        ident16 = sb("ident16", [P, P], BF16)
        ones = sb("ones", [P, P])
        ones16 = sb("ones16", [3, GE], BF16)
        w1a = sb("w1a", [P, H])
        w1b = sb("w1b", [P, H])
        w1c = sb("w1c", [4, H])
        w2s = sb("w2s", [P, H])
        w2h = sb("w2h", [P, H])
        w3s = sb("w3s", [P, 1])
        w3h = sb("w3h", [P, 1])
        wvs = sb("wvs", [P, H])
        brow = sb("brow", [1, 3, H])
        brest = sb("brest", [1, 2, 3, H])
        bparts = sb("bparts", [1, 3, 3, H], BF16)
        bias3 = sb("bias3", [3, 3, H], BF16)
        snd_t = sb("snd_t", [P, T], I32)
        rcv_t = sb("rcv_t", [P, T], I32)
        keyid = sb("keyid", [P, T, 2])
        gidx_t = sb("gidx_t", [P, G, 2 * TPG], I32)
        srow = sb("srow", [P, 2, P, 2])
        nrow = sb("nrow", [P, 2, P, 2])
        key_s = sb("key_s", [P, T])
        next_s = sb("next_s", [P, T])
        id_s = sb("id_s", [P, T], I32)
        sidx_t = sb("sidx_t", [P, T], I32)
        key_g = sb("key_g", [G, GE + 1, 2])
        far_g = sb("far_g", [G, GE], BF16)
        halo = sb("halo", [1, 4])
        rank = sb("rank", [P, T])
        cnt_lt = sb("cnt_lt", [P, T])
        cnt_eq = sb("cnt_eq", [P, T])
        idrel = sb("idrel", [P, T])
        ranki = sb("ranki", [P, T], I32)
        sstage = sb("sstage", [P, TPG, 2])
        sistage = sb("sistage", [P, TPG], I32)
        gidx = sb("gidx", [P, RING, 2 * TPG], I32)
        ridx = sb("ridx", [P, RING, TPG], I32)
        sidx = sb("sidx", [P, RING, TPG], I32)
        hs = sb("hs", [P, RING, TPG, XW])
        rec = sb("rec", [P, RING, TPG, XW])
        back = sb("back", [P, RING, TPG, RW])
        ef = sb("ef", [4, RING, GE])
        far = sb("far", [P, RING, GE], BF16)
        res = sb("res", [P, RING, TPG, H])
        xin = sb("xin", [P, RING, BR, XW])
        xout = sb("xout", [P, XO, BR, H])
        hT = sb("hT", [P, 2, 2, GE])
        th1 = sb("th1", [P, GE])
        x1 = sb("x1", [P, GE])
        th2 = sb("th2", [P, GE])
        x2 = sb("x2", [P, GE])
        shared = sb("shared", [P, 7040])
        at = [0]

        def part(size):
            at[0] += size
            return shared[:, at[0] - size:at[0]]

        mx = part(2 * (GE + 1)).rearrange("p (r e) -> p r e", r=2)
        pa = part(4 * GE).rearrange("p (r a e) -> p r a e", r=2, a=2)
        den = part(2 * GE).rearrange("p (r e) -> p r e", r=2)
        z = part(2 * GE).rearrange("p (r e) -> p r e", r=2)
        at[0] = 0
        hot = part(RING * GE).rearrange("p (r q b) -> p r q b", r=RING, q=TPG)
        hot16 = part(GE).bitcast(BF16).rearrange("p (r q b) -> p r q b", r=2, q=TPG)
        bucket = part(PITCH)
        counts = part(P)
        incl = part(P)
        small = part(P)
        after_placing = at[0]
        placed = part(2 * TPG * CAP).rearrange("p (r q c) -> p r q c", r=2, q=TPG)
        at[0] = after_placing
        other = part(SORTW)
        pick = part(NEAR * ROWLEN).rearrange("p (n j) -> p n j", n=NEAR)
        srt = part(2 * ROWLEN).rearrange("p (j w) -> p j w", w=2)
        parts = part(3 * ROWLEN).rearrange("p (n j) -> p n j", n=3)
        bno = sb("bno", [P, T])
        junk16 = sb("junk16", [P, TPG, P])
        comp = sb("comp", [P, T])
        pos = sb("pos", [P, 2, TPG])
        slot_no = sb("slot_no", [P, CAP])
        before16 = sb("before16", [P, P], BF16)
        after16 = sb("after16", [P, P], BF16)
        all16 = sb("all16", [P, P], BF16)
        cols = sb("cols", [P, 16])
        picki = sb("picki", [P, NEAR], I32)
        flag = sb("flag", [P, 1], I32)
        q_i = sb("q_i", [P, T], I32)
        v, yb = th1, [x1, x2]
        rden = sb("rden", [P, 2, TPG])
        st = sb("st", [P, 2, BR, 6])
        cw = sb("cw", [P, 6, BR])
        rs = sb("rs", [P, 2, 2, BR])

        p_hT = ps("p_hT", [P, 2, GE])
        p_1 = ps("p_1", [P, GE])
        p_2 = ps("p_2", [P, GE])
        p_dt = ps("p_dt", [P, 2, GE])
        p_w = ps("p_w", [P, GE])
        p_m = ps("p_m", [P, TPG, H])

        S = {n: sem(n) for n in (
            "w_in", "t_in", "far_out", "b_in", "setup", "consts_ready", "pool_turn",
            "chunk_in", "chunk_used", "slow", "rank_staged", "rank_scattered", "rank_free", "halo_ready", "halo_out",
            "hot_ready", "cnt_ready", "pos_ready", "placed_ready", "place_done", "buckets_ready", "count_row", "count_col",
            "viol", "viol_sum", "flag_ready", "bucket_out", "pick_ready", "picked", "srt_ready", "srt_out", "hot_made", "rows_taken",
            "sorted_done", "kept", "srt_in", "srt_T", "far_ready",
            "tables_ready", "gidx_ready", "T_ready", "hT_ready", "mm1_done", "th1_ready", "x1_ready", "proj_ready", "rec_msg",
            "mm2_done", "th2_ready", "x2_ready", "s_ready", "rec_s", "rec_written",
            "ridx_ready", "sidx_ready", "sb_ready", "m_ready", "dt_ready", "pa_ready", "mT_ready",
            "v_ready", "z_ready", "agg_ready", "rden_ready", "y_done", "edge_stats", "chain2", "res_ready",
            "dense_stats", "chain1", "norm_done", "norm2_done", "dense_written")}
        hs_in = [sem(f"hs_in{r}") for r in range(RING)]
        hk_in = [sem(f"hk_in{r}") for r in range(RING)]
        ef_in = [sem(f"ef_in{r}") for r in range(RING)]
        far_in = [sem(f"far_in{r}") for r in range(RING)]
        back_in = [sem(f"back_in{r}") for r in range(RING)]
        rec_out = [sem(f"rec_out{r}") for r in range(RING)]
        hk_out = [sem(f"hk_out{r}") for r in range(RING)]
        x_in = [sem(f"x_in{r}") for r in range(RING)]
        stored = [sem(f"stored{r}") for r in range(XO)]
        scattered = [sem(f"scattered{r}") for r in range(RING)]

        block = ctx.enter_context(nc.Block())

        class Turn:

            def __init__(self, k, u):
                self.k, self.u = k, u
                self.fixed = isinstance(k, int)

            def i(self, d=0):
                return self.k * RING + (self.u - d)

            def slot(self, d=0, n=RING):
                return (self.u - d) % n

            def live(self, d=0, count=G):
                return not self.fixed or 0 <= self.i(d) < count

        def wait(eng, s, t, d, per=1, off=0):
            if t.fixed and t.i(d) < 0:
                return
            eng.wait_ge(s, t.i(d) * per + (per + off))

        def wait_round(eng, sems, t, d, per):
            if t.fixed and t.i(d) < 0:
                return
            n = len(sems)
            eng.wait_ge(sems[t.slot(d, n)], t.k * (per * (RING // n)) + (((t.u - d) // n + 1) * per))

        def rounds(eng, body, extra=0):
            for u in range(RING):
                body(Turn(0, u))
            with eng.Fori(1, ROUNDS - 2) as k:
                for u in range(RING):
                    body(Turn(k, u))
            for k in (ROUNDS - 2, ROUNDS - 1):
                for u in range(RING):
                    body(Turn(k, u))
            for u in range(extra):
                body(Turn(ROUNDS, u))

        def column(table, g, fixed):
            return table[:, g * TPG:(g + 1) * TPG] if fixed else table[:, bass.ds(g * TPG, TPG)]

        xflat = xin[:].rearrange("p r b h -> p (r b h)")
        kb_i = xflat[:, 0:CH].bitcast(I32)
        kb = xflat[:, CH:2 * CH]
        jrow = xflat[:, 2 * CH:3 * CH]
        jm = xflat[:, 3 * CH:4 * CH]
        junk = xflat[:, 4 * CH:5 * CH]

        @block.sync
        def _(sp):
            for to, frm in ((snd_t[:], snd_nat), (rcv_t[:], rcv_nat), (idrel[:], id_nat)):
                sp.dma_start(to, frm).then_inc(S["t_in"], 16)
            for to, frm in ((ident[:], eye), (w1a[:], w1[0:H, :]), (w1b[:], w1[H:2 * H, :]), (w1c[:], w1[2 * H:, :]),
                            (w2s[:], w2), (w3s[:], w3), (wvs[:], wv), (brow[:, 0, :], b1), (brow[:, 1, :], b2),
                            (brow[:, 2, :], b3), (slot_no[:], iota[:, 0:CAP].to_broadcast((P, CAP))), (small, tri)):
                sp.dma_start(to, frm).then_inc(S["w_in"], 16)
            sp.wait_ge(S["consts_ready"], 1)
            sp.dma_start(bias3[:], bparts[:]).then_inc(S["b_in"], 16)
            sp.wait_ge(S["halo_ready"], 1)
            sp.dma_start(srt_d[0:1, :], halo[:, 0:2]).then_inc(S["halo_out"], 16)
            sp.dma_start(srt_d[EP + 1:EP + 2, :], halo[:, 2:4]).then_inc(S["halo_out"], 16)

            sp.wait_ge(S["flag_ready"], 1)
            unfit = sp.value_load(flag[0:1, 0:1], min_val=0, max_val=1)
            with sp.If(unfit):
                sp.dma_start(jrow, iota[:, 0:CH].to_broadcast((P, CH))).then_inc(S["chunk_in"], 16)
                with sp.Fori(0, EP // CH) as c:
                    sp.wait_ge(S["chunk_used"], c + 1)
                    sp.dma_start(kb_i, key_row[:, bass.ds(c * CH, CH)].to_broadcast((P, CH))).then_inc(S["chunk_in"], 16)
                sp.wait_ge(S["sorted_done"], 1)

            def sorted_tables():
                with sp.If(unfit):
                    sp.sem_inc(S["kept"], 1)
                with sp.Else():
                    sp.wait_ge(S["srt_ready"], 1)
                    sp.dma_start(srt_d[1:EP + 1, :].rearrange("(p j) w -> p j w", p=P), srt).then_inc(S["srt_out"], 16)
                    sp.wait_ge(S["srt_out"], 16)

                sp.wait_ge(S["halo_out"], 32)
                for to, first in ((srow, 1), (nrow, 2)):
                    sp.dma_start(to[:, 0], srt_d[first:first + P * P, :].rearrange("(t p) w -> t p w", p=P)
                                 ).then_inc(S["srt_in"], 16)
                    sp.dma_start(to[0:T - P, 1], srt_d[first + P * P:first + EP, :].rearrange("(t p) w -> t p w", p=P)
                                 ).then_inc(S["srt_in"], 16)
                sp.dma_start(key_g[:], bass.AP(tensor=srt_d.tensor, offset=0, ap=[[2 * GE, G], [1, 2 * (GE + 1)]])
                             ).then_inc(S["srt_in"], 16)

            def rows_of(t, d):
                if t.fixed and t.i(d) == NB - 1:
                    return slice(LASTROW, N)
                return bass.ds(t.i(d) * BN, BN)

            def load_block(t, d):
                if not t.live(d, NB):
                    return
                if not t.fixed or t.i(d) >= RING:
                    wait(sp, S["norm_done"], t, d + RING)
                    wait(sp, S["norm2_done"], t, d + RING)
                sp.dma_start(xin[:, t.slot(d)], xw[rows_of(t, d), :].rearrange("(p r) h -> p r h", p=P)
                             ).then_inc(x_in[t.slot(d)], 16)

            def load_ef(t, d):
                if not t.live(d, G):
                    return
                wait(sp, S["mm1_done"], t, d + RING)
                sp.dma_start(ef[:, t.slot(d), :], ef_t[:, bass.ds(t.i(d) * GE, GE)]).then_inc(ef_in[t.slot(d)], 16)

            for j in range(AHEAD):
                load_block(Turn(0, j), 0)
                load_ef(Turn(0, j), 0)
            sp.wait_ge(S["buckets_ready"], 1)
            sp.dma_start(buckets_d, bucket).then_inc(S["bucket_out"], 16)

            def body(t):
                if t.live(0):
                    wait_round(sp, hk_in, t, 0, 64)
                    sp.dma_start(rec_d[bass.ds(t.i() * GE, GE), 0:H].rearrange("(q p) w -> p q w", p=P),
                                 back[:, t.slot(), :, 0:H]).then_inc(hk_out[t.slot()], 16)
                if t.live(4):
                    wait(sp, S["rec_s"], t, 4)
                    wait(sp, S["rec_msg"], t, 4)
                    sp.dma_start(rec_d[bass.ds(t.i(4) * GE, GE), H:RW].rearrange("(q p) w -> p q w", p=P),
                                 rec[:, t.slot(4)]).then_inc(rec_out[t.slot(4)], 16)
                load_ef(t, -AHEAD)
                load_block(t, -AHEAD)
                if t.live(2, NB):
                    wait(sp, S["norm_done"], t, 2)
                    wait(sp, S["norm2_done"], t, 2)
                    if t.fixed and t.i(2) == NB - 1:
                        wait_round(sp, stored, t, 3, 16)
                    sp.dma_start(out[rows_of(t, 2), :].rearrange("(p r) h -> p r h", p=P), xout[:, t.slot(2, XO)]
                                 ).then_inc(stored[t.slot(2, XO)], 16)
                if t.fixed and t.i() == 2:
                    sorted_tables()

            rounds(sp, body, 1)
            for r in range(XO):
                sp.wait_ge(stored[r], 16 * len(range(r, NB, XO)))
            sp.sem_inc(S["dense_written"], 1)
            for r in range(RING):
                sp.wait_ge(rec_out[r], 16 * len(range(r, G, RING)))
                sp.wait_ge(hk_out[r], 16 * len(range(r, G, RING)))
            sp.sem_inc(S["rec_written"], 1)

            sp.wait_ge(S["far_ready"], 1)
            sp.dma_start(far_d, far_g[:]).then_inc(S["far_out"], 16)
            sp.wait_ge(S["far_out"], 16)

            def load_far(t, d):
                if not t.live(d, G):
                    return
                wait(sp, S["m_ready"], t, d + RING)
                wait(sp, S["dt_ready"], t, d + RING)
                sp.dma_start(far[:, t.slot(d), :], far_d[bass.ds(t.i(d), 1), :].to_broadcast((P, GE))
                             ).then_inc(far_in[t.slot(d)], 16)

            for j in range(AHEAD):
                load_far(Turn(0, j), 0)
            rounds(sp, lambda t: load_far(t, -AHEAD))

        @block.gpsimd
        def _(pool):
            def rows_in(to, index, sems, r):
                for q in range(TPG):
                    pool.indirect_dma_start(out=to(q), out_offset=None, in_=xw,
                                            in_offset=bass.IndirectOffsetOnAxis(ap=index(q), axis=0)).then_inc(sems[r], 16)

            def sort_moves():
                pool.wait_ge(S["flag_ready"], 1)
                unfit = pool.value_load(flag[0:1, 0:1], min_val=0, max_val=1)
                with pool.If(unfit):
                    pool.sem_inc(S["rank_free"], 1)
                    with pool.Fori(0, G) as g:
                        pool.wait_ge(S["rank_staged"], g + 1)
                        pool.sem_inc(S["pool_turn"], 1)
                        for q in range(TPG):
                            pool.indirect_dma_start(
                                out=srt_d, out_offset=bass.IndirectOffsetOnAxis(ap=sistage[:, q:q + 1], axis=0),
                                in_=sstage[:, q, :], in_offset=None, bounds_check=EP, oob_is_err=False
                            ).then_inc(S["rank_scattered"], 16)
                        pool.wait_ge(S["rank_scattered"], (g + 1) * (16 * TPG))
                        pool.sem_inc(S["rank_free"], 1)
                    pool.sem_inc(S["sorted_done"], 1)
                pool.wait_ge(S["bucket_out"], 16)
                pool.wait_ge(S["pick_ready"], 1)
                for n in range(NEAR):
                    pool.indirect_dma_start(out=pick[:, n, :], out_offset=None, in_=buckets_d,
                                            in_offset=bass.IndirectOffsetOnAxis(ap=picki[:, n:n + 1], axis=1)
                                            ).then_inc(S["picked"], 16)

            def gather(t, d):
                if not t.live(d, G):
                    return
                r = t.slot(d)
                wait(pool, S["gidx_ready"], t, d)
                wait(pool, S["T_ready"], t, d + RING)
                wait(pool, S["rec_msg"], t, d + RING)
                pool.sem_inc(S["pool_turn"], 1)
                rows_in(lambda q: hs[:, r, q, :], lambda q: gidx[:, r, TPG + q:TPG + q + 1], hs_in, r)
                wait_round(pool, hk_out, t, d + RING, 16)
                pool.sem_inc(S["pool_turn"], 1)
                rows_in(lambda q: back[:, r, q, 0:XW], lambda q: gidx[:, r, q:q + 1], hk_in, r)

            for j in range(RING):
                gather(Turn(0, j), 0)
            sort_moves()
            rounds(pool, lambda t: None if t.fixed and t.i(-AHEAD) < RING else gather(t, -AHEAD))

            def gather_back(t, d):
                if not t.live(d, G):
                    return
                r = t.slot(d)
                wait(pool, S["ridx_ready"], t, d)
                wait(pool, S["y_done"], t, d + RING, per=TPG)
                pool.sem_inc(S["pool_turn"], 1)
                for q in range(TPG):
                    pool.indirect_dma_start(
                        out=back[:, r, q, :], out_offset=None, in_=rec_d,
                        in_offset=bass.IndirectOffsetOnAxis(ap=ridx[:, r, q:q + 1], axis=0)).then_inc(back_in[r], 16)

            def scatter(t, d):
                if not t.live(d, G):
                    return
                r = t.slot(d)
                wait(pool, S["res_ready"], t, d)
                wait(pool, S["sidx_ready"], t, d)
                pool.sem_inc(S["pool_turn"], 1)
                for q in range(TPG):
                    pool.indirect_dma_start(
                        out=out, out_offset=bass.IndirectOffsetOnAxis(ap=sidx[:, r, q:q + 1], axis=0),
                        in_=res[:, r, q, :], in_offset=None, bounds_check=N - 1, oob_is_err=False
                    ).then_inc(scattered[r], 16)

            pool.wait_ge(S["rec_written"], 1)
            for j in range(AHEAD):
                gather_back(Turn(0, j), 0)
            pool.wait_ge(S["dense_written"], 1)

            def body2(t):
                gather_back(t, -AHEAD)
                scatter(t, 4)

            rounds(pool, body2, 1)
            for r in range(RING):
                pool.wait_ge(scattered[r], 16 * TPG * len(range(r, G, RING)))

        @block.scalar
        def _(act):
            def sort_body(t):
                if t.live(0):
                    wait(act, S["hot_made"], t, 0)
                    wait(act, S["pos_ready"], t, 1)
                    wait(act, S["cnt_ready"], t, 1)
                    nc.scalar.activation(hot16[:, t.slot(0, 2)], hot[:, t.slot()], ACT.Copy).then_inc(S["hot_ready"], 1)

            rounds(act, sort_body)

            def dense_norm(t, d, lo, hi):
                if not t.live(d, NB):
                    return
                if lo == 0:
                    wait(act, S["chain1"], t, d, per=STEPS)
                    wait_round(act, stored, t, d + XO, 16)
                    wait_round(act, x_in, t, d, 16)
                for j in range(lo, hi):
                    ins = nc.scalar.activation(xout[:, t.slot(d, XO), j, :], xin[:, t.slot(d), j, 0:H], ACT.Identity,
                                               bias=rs[:, t.slot(d, 2), 1, j:j + 1], scale=rs[:, t.slot(d, 2), 0, j:j + 1])
                if hi == ACT_ROWS:
                    ins.then_inc(S["norm_done"], 1)

            def body(t):
                if t.live(3):
                    wait(act, S["mm2_done"], t, 3)
                    wait(act, S["x2_ready"], t, 4)
                    nc.scalar.activation(th2[:], p_2[:], ACT.Tanh, scale=0.5).then_inc(S["th2_ready"], 1)
                dense_norm(t, 2, 0, 4)
                if t.live(0):
                    wait(act, S["T_ready"], t, 0)
                    wait(act, S["mm1_done"], t, 2)
                    wait(act, S["proj_ready"], t, 2)
                    nc.scalar.activation(hT[:, t.slot(0, 2)], p_hT[:], ACT.Copy).then_inc(S["hT_ready"], 1)
                dense_norm(t, 2, 4, 9)
                if t.live(1):
                    wait(act, S["mm1_done"], t, 1)
                    wait(act, S["x1_ready"], t, 2)
                    nc.scalar.activation(th1[:], p_1[:], ACT.Tanh, scale=0.5).then_inc(S["th1_ready"], 1)
                dense_norm(t, 2, 9, ACT_ROWS)

            rounds(act, body, 1)

            def body2(t):
                if t.live(0):
                    wait(act, S["dt_ready"], t, 0)
                    wait(act, S["z_ready"], t, 2)
                    nc.scalar.activation(pa[:, t.slot(0, 2)], p_dt[:], ACT.Exp).then_inc(S["pa_ready"], 1)
                if t.live(3):
                    wait(act, S["chain2"], t, 3, per=STEPS)
                    wait(act, S["y_done"], t, 3, per=TPG)
                    wait_round(act, scattered, t, 3 + RING, 64)
                    for q in range(TPG):
                        ins = nc.scalar.activation(res[:, t.slot(3), q, :], yb[t.slot(3, 2)][:, q * H:(q + 1) * H],
                                                   ACT.Identity, scale=rs[:, t.slot(3, 2), 0, q:q + 1],
                                                   bias=rs[:, t.slot(3, 2), 1, q:q + 1])
                    ins.then_inc(S["res_ready"], 1)

            rounds(act, body2, 1)

        @block.tensor
        def _(pe):
            pe.wait_ge(S["w_in"], 192)
            pe.wait_ge(S["consts_ready"], 2)
            p_cnt = p_dt[:, 0, :].rearrange("p (q b) -> p q b", q=TPG)
            p_place = p_w[:, 0:CAP]

            def sort_body(t):
                if t.live(1):
                    wait(pe, S["pos_ready"], t, 1)
                    for q in range(TPG):
                        for o in range(q, TPG):
                            pe.matmul(p_cnt[:, q, :], after16[:] if o == q else all16[:], hot16[:, t.slot(1, 2), o, :],
                                      start=False, stop=True, skip_group_check=True)
                if t.live(0):
                    wait(pe, S["hot_ready"], t, 0)
                    for q in range(TPG):
                        for o in range(q + 1):
                            first = t.fixed and t.i() == 0 and q == 0
                            ins = pe.matmul(p_cnt[:, q, :], before16[:] if o == q else all16[:], hot16[:, t.slot(0, 2), o, :],
                                            start=first, stop=True, skip_group_check=True)
                    ins.then_inc(S["cnt_ready"], 1)
                if t.live(1):
                    wait(pe, S["placed_ready"], t, 1)
                    for q in range(TPG):
                        first = t.fixed and t.i(1) == 0 and q == 0
                        ins = pe.matmul(p_place, hot[:, t.slot(1), q, :], placed[:, t.slot(1, 2), q, :], start=first, stop=True,
                                        skip_group_check=True)
                    ins.then_inc(S["place_done"], 1)

            rounds(pe, sort_body)
            pe.wait_ge(S["count_row"], 1)
            pe.matmul(p_1[:, 0:1], counts, ident[:, 0:1], start=True, stop=True).then_inc(S["count_col"], 1)
            pe.wait_ge(S["viol"], 1)
            pe.matmul(p_2[:, 0:1], ones[:], cols[:, 0:1], start=True, stop=True).then_inc(S["viol_sum"], 1)

            pe.wait_ge(S["b_in"], 16)
            pe.wait_ge(S["rows_taken"], 1)

            def body(t):
                if t.live(0):
                    wait(pe, S["hT_ready"], t, 1)
                    wait_round(pe, hs_in, t, 0, 64)
                    for q in range(TPG):
                        pe.transpose(p_hT[:, 1, q * P:(q + 1) * P], hs[:, t.slot(), q, 0:H], ident[:])
                    wait_round(pe, hk_in, t, 0, 64)
                    for q in range(TPG):
                        ins = pe.transpose(p_hT[:, 0, q * P:(q + 1) * P], back[:, t.slot(), q, 0:H], ident[:])
                    ins.then_inc(S["T_ready"], 1)
                if t.live(1):
                    h = hT[:, t.slot(1, 2)]
                    wait(pe, S["hT_ready"], t, 1)
                    wait(pe, S["x1_ready"], t, 2)
                    wait_round(pe, ef_in, t, 1, 16)
                    pe.matmul(p_1[:], w1a[:], h[:, 0, :], start=True, stop=False)
                    pe.matmul(p_1[:], w1b[:], h[:, 1, :], start=False, stop=False)
                    pe.matmul(p_1[:], w1c[:], ef[:, t.slot(1), :], start=False, stop=False)
                    pe.matmul(p_1[:], bias3[:, 0, :], ones16[:], start=False, stop=True).then_inc(S["mm1_done"], 1)
                    wait(pe, S["rec_msg"], t, 2)
                    for q in range(TPG):
                        ins = pe.matmul(p_m[:, q, :], h[:, 1, q * P:(q + 1) * P], wvs[:], start=True, stop=True)
                    ins.then_inc(S["proj_ready"], 1)
                if t.live(2):
                    wait(pe, S["x1_ready"], t, 2)
                    wait(pe, S["x2_ready"], t, 3)
                    pe.matmul(p_2[:], w2h[:], x1[:], start=True, stop=False)
                    pe.matmul(p_2[:], bias3[:, 1, :], ones16[:], start=False, stop=True).then_inc(S["mm2_done"], 1)
                if t.live(3):
                    wait(pe, S["x2_ready"], t, 3)
                    wait(pe, S["rec_s"], t, 4)
                    for q in range(TPG):
                        pe.matmul(p_w[:, q:q + 1], x2[:, q * P:(q + 1) * P], w3h[:], start=True, stop=False)
                        ins = pe.matmul(p_w[:, q:q + 1], ones16[:, 0:P], bias3[:, 2, 0:1], start=False, stop=True)
                    ins.then_inc(S["s_ready"], 1)
                if t.fixed and t.i() == 3:
                    pe.wait_ge(S["srt_in"], 80)
                    for n, (row, w, to) in enumerate(((srow, 0, p_dt[:, 0, 0:T]), (nrow, 0, p_dt[:, 1, 0:T]), (srow, 1, p_dt[:, 1, T:2 * T]))):
                        pe.transpose(to[:, 0:P], row[:, 0, :, w], ident[:])
                        pe.transpose(to[:, P:T], row[0:T - P, 1, :, w], ident[0:T - P, 0:T - P]).then_inc(S["srt_T"], 1)

            rounds(pe, body, 1)
            pe.wait_ge(S["tables_ready"], 1)

            def body2(t):
                if t.live(0):
                    wait_round(pe, back_in, t, 0, 64)
                    wait(pe, S["pa_ready"], t, 1)
                    for q in range(TPG):
                        ins = pe.matmul(p_dt[:, 0, q * P:(q + 1) * P],
                                        back[:, t.slot(), q, RW - 1:RW].to_broadcast((P, P)), ident[:],
                                        start=(q == 0), stop=True, skip_group_check=True)
                    ins.then_inc(S["sb_ready"], 1)
                if t.live(1):
                    wait_round(pe, back_in, t, 1, 64)
                    wait(pe, S["v_ready"], t, 2)
                    for q in range(TPG):
                        ins = pe.transpose(p_w[:, q * P:(q + 1) * P], back[:, t.slot(1), q, H:2 * H], ident[:])
                    ins.then_inc(S["mT_ready"], 1)
                if t.live(0):
                    wait(pe, S["m_ready"], t, 0)
                    wait_round(pe, far_in, t, 0, 16)
                    m = mx[:, t.slot(0, 2), :]
                    pe.matmul(p_dt[:, 0, :], nident[:], m[:, 1:GE + 1], start=False, stop=True, skip_group_check=True)
                    pe.matmul(p_dt[:, 1, :], ident16[:], far[:, t.slot(), :], start=True, stop=False)
                    pe.matmul(p_dt[:, 1, :], ident[:], m[:, 0:GE], start=False, stop=False)
                    pe.matmul(p_dt[:, 1, :], nident[:], m[:, 1:GE + 1], start=False, stop=True).then_inc(S["dt_ready"], 1)
                if t.live(1):
                    wait(pe, S["z_ready"], t, 1)
                    wait(pe, S["y_done"], t, 2, per=TPG)
                    for q in range(TPG):
                        pe.matmul(p_2[:, q:q + 1], den[0:1, t.slot(1, 2), q * P:(q + 1) * P], ones[0:1, 0:1],
                                  start=True, stop=True)
                    for q in range(TPG):
                        ins = pe.transpose(p_m[:, q, :], z[:, t.slot(1, 2), q * P:(q + 1) * P], ident[:])
                    ins.then_inc(S["agg_ready"], 1)

            rounds(pe, body2)

        @block.vector
        def _(dve):
            vec = nc.vector
            count = [0]

            def link(ins, s="setup"):
                count[0] += 1
                ins.then_inc(S[s], 1)
                dve.wait_ge(S[s], count[0])

            dve.wait_ge(S["t_in"], 48)
            vec.tensor_scalar(gidx_t[:, :, 0:TPG], rcv_t[:].rearrange("p (g q) -> p g q", q=TPG), float(N - 1), None, ALU.min)
            vec.tensor_copy(gidx_t[:, :, TPG:2 * TPG], snd_t[:].rearrange("p (g q) -> p g q", q=TPG))
            vec.tensor_copy(keyid[:, :, 0], rcv_t[:])
            vec.tensor_copy(keyid[:, :, 1], idrel[:])
            vec.memset(rank[:], 1.0)
            vec.memset(cnt_lt[:], 0.0)
            vec.memset(cnt_eq[:], 0.0)
            vec.memset(halo[:, 0:2], -1.0)
            link(vec.memset(halo[:, 2:4], float(N + 1)))
            vec.memset(ones[:], 1.0).then_inc(S["halo_ready"], 1)
            vec.tensor_scalar(ranki[:], rcv_t[:], 10, None, ALU.logical_shift_right)
            link(vec.tensor_scalar(q_i[:], rcv_t[:], BUCKET - 1, None, ALU.bitwise_and))
            vec.tensor_copy(bno[:], ranki[:])
            link(vec.tensor_scalar(comp[:], q_i[:], -float(BUCKET // 2), float(EP), ALU.add, ALU.mult))
            link(vec.tensor_tensor(comp[:], comp[:], idrel[:], ALU.add))
            vec.memset(ones16[:], 1.0)
            dve.wait_ge(S["w_in"], 192)
            vec.tensor_scalar(nident[:], ident[:], -1.0, None, ALU.mult)
            vec.tensor_copy(ident16[:], ident[:])
            vec.tensor_scalar(w2h[:], w2s[:], 0.5, None, ALU.mult)
            vec.tensor_scalar(w3h[:], w3s[:], 0.5, None, ALU.mult)
            link(vec.tensor_copy(bparts[:, 0], brow[:]))
            link(vec.tensor_tensor(brest[:, 0], brow[:], bparts[:, 0], ALU.subtract))
            link(vec.tensor_copy(bparts[:, 1], brest[:, 0]))
            link(vec.tensor_tensor(brest[:, 1], brest[:, 0], bparts[:, 1], ALU.subtract))
            link(vec.tensor_copy(bparts[:, 2], brest[:, 1]))
            link(vec.memset(cw[:], 1.0))
            link(vec.memset(cols[:], 0.0))
            dve.sem_inc(S["consts_ready"], 2)

            def copy_gidx(t, d):
                if t.live(d, G):
                    wait_round(dve, hk_in, t, d + RING, 64)
                    wait_round(dve, hs_in, t, d + RING, 64)
                    g = t.i(d)
                    at = gidx_t[:, g, :] if t.fixed else gidx_t[:, bass.ds(g, 1), :].rearrange("p a q -> p (a q)")
                    vec.tensor_copy(gidx[:, t.slot(d), :], at).then_inc(S["gidx_ready"], 1)

            for j in range(RING):
                copy_gidx(Turn(0, j), 0)

            vec.memset(all16[:], 1.0)
            vec.tensor_copy(before16[:], small)
            vec.tensor_scalar(after16[:], small, -1.0, 1.0, ALU.mult, ALU.add)
            vec.memset(bucket, BIG)

            def sort_body(t):
                if t.live(0):
                    wait(dve, S["place_done"], t, RING)
                    wait(dve, S["hot_ready"], t, RING)
                    for q in range(TPG):
                        ins = vec.tensor_scalar(hot[:, t.slot(), q, :], slot_no[:, 0:P],
                                                bno[:, bass.ds(t.i() * TPG + q, 1)], None, ALU.is_equal)
                    ins.then_inc(S["hot_made"], 1)
                if t.live(1):
                    wait(dve, S["cnt_ready"], t, 1)
                    wait(dve, S["hot_made"], t, 1)
                    wait(dve, S["placed_ready"], t, 2)
                    for q in range(TPG):
                        ins = vec.tensor_tensor_reduce(junk16[:, q, :], p_dt[:, 0, q * P:(q + 1) * P], hot[:, t.slot(1), q, :],
                                                       1.0, 0.0, ALU.mult, ALU.add, pos[:, t.slot(1, 2), q:q + 1])
                    ins.then_inc(S["pos_ready"], 1)
                if t.live(1):
                    wait(dve, S["pos_ready"], t, 1)
                    wait(dve, S["place_done"], t, 3)
                    for q in range(TPG):
                        ins = vec.tensor_scalar(placed[:, t.slot(1, 2), q, :], slot_no[:], pos[:, t.slot(1, 2), q:q + 1],
                                                comp[:, bass.ds(t.i(1) * TPG + q, 1)], ALU.is_equal, ALU.mult)
                    ins.then_inc(S["placed_ready"], 1)

            rounds(dve, sort_body)
            dve.wait_ge(S["place_done"], G)
            link(vec.tensor_copy(counts, p_dt[:, 0, 0:P]))
            dve.sem_inc(S["count_row"], 1)
            sc = {n: cols[:, m:m + 1] for m, n in enumerate(
                ("viol", "start", "end", "b0", "b1", "most", "unfit", "bk", "base", "off"))}
            link(vec.tensor_tensor_scan(incl, ones[:], counts, 0.0, ALU.mult, ALU.add))
            link(vec.tensor_scalar(sc["start"], idrel[:, 0:1], float(ROWLEN), None, ALU.mult))
            link(vec.tensor_scalar(sc["end"], sc["start"], float(ROWLEN - 1), None, ALU.add))
            link(vec.tensor_scalar(small, incl, sc["start"], None, ALU.is_le))
            link(vec.tensor_reduce(sc["b0"], small, mybir.AxisListType.X, ALU.add))
            link(vec.tensor_scalar(small, incl, sc["end"], None, ALU.is_le))
            link(vec.tensor_reduce(sc["b1"], small, mybir.AxisListType.X, ALU.add))
            link(vec.tensor_reduce(sc["most"], counts, mybir.AxisListType.X, ALU.max))
            link(vec.tensor_tensor(sc["b1"], sc["b1"], sc["b0"], ALU.subtract))
            link(vec.tensor_scalar(sc["unfit"], sc["b1"], float(NEAR - 1), None, ALU.is_gt))
            link(vec.tensor_scalar(sc["most"], sc["most"], float(CAP), None, ALU.is_gt))
            link(vec.tensor_tensor(sc["viol"], sc["most"], sc["unfit"], ALU.add))
            dve.sem_inc(S["viol"], 1)
            for n in range(NEAR):
                link(vec.tensor_scalar(sc["bk"], sc["b0"], float(n), None, ALU.add))
                link(vec.scalar_tensor_tensor(out=small, in0=slot_no[:, 0:P], scalar=sc["bk"], in1=counts, op0=ALU.is_lt,
                                              op1=ALU.mult))
                link(vec.tensor_reduce(sc["base"], small, mybir.AxisListType.X, ALU.add))
                link(vec.tensor_tensor(sc["off"], sc["start"], sc["base"], ALU.subtract))
                link(vec.tensor_scalar(sc["off"], sc["off"], -float(ROWLEN + 4), float(PAD), ALU.max, ALU.add))
                link(vec.tensor_scalar(sc["off"], sc["off"], float(CAP + PAD), None, ALU.min))
                link(vec.scalar_tensor_tensor(out=sc["off"], in0=sc["bk"], scalar=float(PITCH), in1=sc["off"], op0=ALU.mult,
                                              op1=ALU.add))
                link(vec.tensor_copy(picki[:, n:n + 1], sc["off"]))
            dve.sem_inc(S["pick_ready"], 1)
            dve.wait_ge(S["viol_sum"], 1)
            link(vec.tensor_scalar(flag[:], p_2[:, 0:1], 0.5, None, ALU.is_gt))
            dve.sem_inc(S["flag_ready"], 1)

            dve.wait_ge(S["count_col"], 1)
            link(vec.tensor_scalar(other[:, 0:CAP], slot_no[:], p_1[:, 0:1], BIG, ALU.is_ge, ALU.mult))
            row = bucket[:, PAD:PAD + SORTW]
            vec.memset(other[:, SORTW * 3 // 4:], BIG)
            link(vec.tensor_tensor(row[:, 0:CAP], p_w[:, 0:CAP], other[:, 0:CAP], ALU.add))
            dve.sem_inc(S["rows_taken"], 1)
            frm, to = row, other
            k = 2
            while k <= SORTW:
                j = k // 2
                while j:
                    wide = SORTW * 3 // 4 if k <= SORTW // 8 else SORTW

                    def halves(x, down):
                        x = x[:, 0:wide]
                        if k == SORTW:
                            w = x.rearrange("p (c two j) -> p c two j", two=2, j=j)
                            return w[:, :, 0, :], w[:, :, 1, :]
                        w = x.rearrange("p (m d k) -> p m d k", d=2, k=k)[:, :, down, :]
                        w = w.rearrange("p m (c two j) -> p m c two j", two=2, j=j)
                        return w[:, :, :, 0, :], w[:, :, :, 1, :]
                    for down in range(1 if k == SORTW else 2):
                        lo, hi = halves(frm, down)
                        tlo, thi = halves(to, down)
                        vec.tensor_tensor(tlo, lo, hi, ALU.max if down else ALU.min)
                        ins = vec.tensor_tensor(thi, lo, hi, ALU.min if down else ALU.max)
                    link(ins)
                    frm, to = to, frm
                    j //= 2
                k *= 2
            if frm is not row:
                link(vec.tensor_copy(row, frm))
            dve.sem_inc(S["buckets_ready"], 1)

            unfit = dve.value_load(flag[0:1, 0:1], min_val=0, max_val=1)
            with dve.If(unfit):
                vec.memset(junk, 0.0).then_inc(S["chunk_used"], 1)
                per = 3 + 3 * T
                with dve.Fori(0, EP // CH) as c:
                    dve.wait_ge(S["chunk_in"], c * 16 + 32)
                    vec.tensor_copy(kb, kb_i).then_inc(S["slow"], 1)
                    dve.wait_ge(S["slow"], c * per + 1)
                    vec.memset(cw[:, 0, 1:2], 1.0)
                    with dve.Fori(0, T) as t:
                        base = c * per + t * 3 + 1
                        key = keyid[:, bass.ds(t, 1), 0]
                        vec.tensor_scalar(junk, kb, key, 0.0, ALU.is_lt, ALU.add, accum_out=cnt_lt[:, bass.ds(t, 1)])
                        vec.tensor_scalar(jm, jrow, idrel[:, bass.ds(t, 1)], None, ALU.is_lt).then_inc(S["slow"], 1)
                        dve.wait_ge(S["slow"], base + 1)
                        vec.scalar_tensor_tensor(out=junk, in0=kb, scalar=key, in1=jm, op0=ALU.is_equal, op1=ALU.mult
                                                 ).then_inc(S["slow"], 1)
                        dve.wait_ge(S["slow"], base + 2)
                        vec.tensor_reduce(cnt_eq[:, bass.ds(t, 1)], junk, mybir.AxisListType.X, ALU.add).then_inc(S["slow"], 1)
                        dve.wait_ge(S["slow"], base + 3)
                    vec.tensor_tensor(rank[:], rank[:], cnt_lt[:], ALU.add).then_inc(S["slow"], 1)
                    dve.wait_ge(S["slow"], c * per + (3 * T + 2))
                    vec.tensor_scalar(idrel[:], idrel[:], -float(CH), None, ALU.add)
                    vec.tensor_tensor(rank[:], rank[:], cnt_eq[:], ALU.add).then_inc(S["slow"], 1)
                    dve.wait_ge(S["slow"], c * per + (3 * T + 3))
                    vec.memset(cw[:, 0, 0:1], 1.0).then_inc(S["chunk_used"], 1)
                vec.tensor_copy(ranki[:], rank[:]).then_inc(S["slow"], 1)
                dve.wait_ge(S["slow"], (EP // CH) * (3 + 3 * T) + 1)
                with dve.Fori(0, G) as g:
                    with_g = bass.ds(g * TPG, TPG)
                    dve.wait_ge(S["rank_free"], g + 1)
                    vec.tensor_copy(sistage[:], ranki[:, with_g])
                    vec.tensor_copy(sstage[:], keyid[:, with_g, :]).then_inc(S["rank_staged"], 1)


            def decode():
                dve.wait_ge(S["picked"], 16 * NEAR)
                val, bq, qf, idd, t1 = srt[:, :, 0], srt[:, :, 1], parts[:, 0, :], parts[:, 1, :], parts[:, 2, :]
                link(vec.tensor_tensor(val, pick[:, 0, :], pick[:, 1, :], ALU.min))
                for n in range(2, NEAR):
                    link(vec.tensor_tensor(val, val, pick[:, n, :], ALU.min))
                for n in range(1, NEAR):
                    link(vec.tensor_scalar(pick[:, n, :], pick[:, n, :], BIG / 2, float(n), ALU.is_lt, ALU.mult))
                link(vec.tensor_tensor(bq, pick[:, 1, :], pick[:, 2, :], ALU.add))
                link(vec.tensor_scalar(bq, bq, sc["b0"], float(BUCKET), ALU.add, ALU.mult))
                link(vec.tensor_scalar(q_i[:], val, 1.0 / EP, None, ALU.mult))
                link(vec.tensor_copy(qf, q_i[:]))
                link(vec.scalar_tensor_tensor(out=idd, in0=qf, scalar=-float(EP), in1=val, op0=ALU.mult, op1=ALU.add))
                link(vec.tensor_scalar(t1, idd, 0.0, None, ALU.is_lt))
                link(vec.tensor_tensor(qf, qf, t1, ALU.subtract))
                link(vec.scalar_tensor_tensor(out=idd, in0=t1, scalar=float(EP), in1=idd, op0=ALU.mult, op1=ALU.add))
                link(vec.tensor_scalar(t1, idd, float(EP), None, ALU.is_ge))
                link(vec.tensor_tensor(qf, qf, t1, ALU.add))
                link(vec.scalar_tensor_tensor(out=t1, in0=t1, scalar=-float(EP), in1=idd, op0=ALU.mult, op1=ALU.add))
                link(vec.tensor_scalar(qf, qf, float(BUCKET // 2), None, ALU.add))
                link(vec.tensor_tensor(qf, bq, qf, ALU.add))
                link(vec.tensor_copy(srt[:, :, 0], qf))
                link(vec.tensor_copy(srt[:, :, 1], t1))
                dve.sem_inc(S["srt_ready"], 1)

            def index_tables():
                dve.wait_ge(S["srt_in"], 80)
                link(vec.tensor_tensor(far_g[:], key_g[:, 1:GE + 1, 0], key_g[:, 0:GE, 0], ALU.not_equal))
                link(vec.tensor_scalar(far_g[:], far_g[:], FAR, None, ALU.mult))
                dve.sem_inc(S["far_ready"], 1)
                dve.wait_ge(S["srt_T"], 3)
                vec.tensor_copy(id_s[:], p_dt[:, 1, T:2 * T])
                link(vec.tensor_copy(key_s[:], p_dt[:, 0, 0:T]))
                link(vec.tensor_tensor(next_s[:], key_s[:], p_dt[:, 1, 0:T], ALU.is_equal))
                link(vec.scalar_tensor_tensor(out=sidx_t[:], in0=next_s[:], scalar=SKIP, in1=key_s[:], op0=ALU.mult, op1=ALU.add))

            def chain(t, d, n, s, o, step_sem, stats_sem, gate):
                sm, dl, q, va, a, b = (cw[:, m, 0:n] for m in range(6))
                r, bi = o[:, 0, 0:n], o[:, 1, 0:n]
                ri, vi, ai = r.bitcast(I32), va.bitcast(I32), a.bitcast(I32)
                s = s[:, 0:n, :]

                def step(ins):
                    ins.then_inc(step_sem, 1)

                def after(m):
                    wait(dve, step_sem, t, d, per=STEPS, off=m - STEPS)

                wait(dve, stats_sem, t, d)
                step(vec.tensor_tensor(dl, s[:, :, 1], s[:, :, 4], ALU.subtract)); yield
                step(vec.tensor_tensor(sm, s[:, :, 1], s[:, :, 4], ALU.add)); yield
                step(vec.tensor_tensor(q, s[:, :, 2], s[:, :, 5], ALU.add)); yield
                after(1)
                step(vec.tensor_tensor(a, dl, dl, ALU.mult)); yield
                after(4)
                step(vec.scalar_tensor_tensor(out=b, in0=a, scalar=32.0, in1=q, op0=ALU.mult, op1=ALU.add)); yield
                after(5)
                step(vec.tensor_scalar(va, b, 1.0 / H, EPS_LN / 4, ALU.mult, ALU.add)); yield
                after(6)
                step(vec.tensor_scalar(ai, vi, 1, None, ALU.logical_shift_right)); yield
                after(7)
                gate()
                step(vec.tensor_scalar(ri, ai, -1.0, MAGIC, ALU.mult, ALU.add)); yield
                for m in range(3):
                    after(8 + 3 * m)
                    step(vec.scalar_tensor_tensor(out=a, in0=r, scalar=-0.5, in1=r, op0=ALU.mult, op1=ALU.mult)); yield
                    after(9 + 3 * m)
                    step(vec.tensor_tensor(b, a, va, ALU.mult)); yield
                    after(10 + 3 * m)
                    step(vec.scalar_tensor_tensor(out=r, in0=b, scalar=1.5, in1=r, op0=ALU.add, op1=ALU.mult)); yield
                after(17)
                step(vec.scalar_tensor_tensor(out=bi, in0=sm, scalar=-0.5, in1=r, op0=ALU.mult, op1=ALU.mult)); yield
                after(18)

            def body(t):
                def gate():
                    if t.live(3, NB):
                        wait(dve, S["norm_done"], t, 3)

                steps = iter(())
                if t.live(1, NB):
                    steps = chain(t, 1, BR, st[:, t.slot(1, 2)], rs[:, t.slot(1, 2)], S["chain1"], S["dense_stats"], gate)

                def more(n=1):
                    for _ in range(n):
                        next(steps, None)

                def stats(lo, hi):
                    if not t.live(0, NB):
                        return
                    if lo == 0:
                        wait_round(dve, x_in, t, 0, 16)
                    for j in range(lo, hi):
                        ins = vec.bn_stats(st[:, t.slot(0, 2), j, :], xin[:, t.slot(), j, 0:H])
                        if j == BR - 1:
                            ins.then_inc(S["dense_stats"], 1)
                        more()

                if not (t.fixed and t.i(-AHEAD) < RING):
                    copy_gidx(t, -AHEAD)
                if t.live(4):
                    wait(dve, S["s_ready"], t, 4)
                    wait_round(dve, rec_out, t, 4 + RING, 16)
                    vec.tensor_copy(rec[:, t.slot(4), :, H], p_w[:, 0:TPG]).then_inc(S["rec_s"], 1)
                stats(0, 1)
                if t.live(3):
                    wait(dve, S["th2_ready"], t, 3)
                    wait(dve, S["s_ready"], t, 4)
                    vec.scalar_tensor_tensor(out=x2[:], in0=th2[:], scalar=1.0, in1=p_2[:], op0=ALU.add, op1=ALU.mult
                                             ).then_inc(S["x2_ready"], 1)
                more()
                stats(1, 10)
                if t.live(1):
                    wait(dve, S["th1_ready"], t, 1)
                    wait(dve, S["mm2_done"], t, 2)
                    vec.scalar_tensor_tensor(out=x1[:], in0=th1[:], scalar=1.0, in1=p_1[:], op0=ALU.add, op1=ALU.mult
                                             ).then_inc(S["x1_ready"], 1)
                more()
                stats(10, 13)
                if t.live(1):
                    wait(dve, S["proj_ready"], t, 1)
                    wait_round(dve, rec_out, t, 1 + RING, 16)
                    w = hs[:, t.slot(1), :, H:H + 1].to_broadcast((P, TPG, H))
                    vec.tensor_tensor(rec[:, t.slot(1), :, 0:H], p_m[:], w, ALU.mult).then_inc(S["rec_msg"], 1)
                stats(13, BR)
                if t.live(2, NB):
                    wait(dve, S["chain1"], t, 2, per=STEPS)
                    wait_round(dve, stored, t, 2 + XO, 16)
                    for j in range(ACT_ROWS, BR):
                        ins = vec.tensor_scalar(xout[:, t.slot(2, XO), j, :], xin[:, t.slot(2), j, 0:H],
                                                rs[:, t.slot(2, 2), 0, j:j + 1], rs[:, t.slot(2, 2), 1, j:j + 1],
                                                ALU.mult, ALU.add)
                    ins.then_inc(S["norm2_done"], 1)
                more(99)
                if t.fixed and t.i() == 1:
                    decode()
                if t.fixed and t.i() == 3:
                    index_tables()

            rounds(dve, body, 1)
            vec.memset(mx[:, 0, 0:1], 0.0)
            vec.memset(den[:, 1, GE - 1:GE], 0.0)
            vec.memset(z[:, 1, GE - 1:GE], 0.0)
            vec.memset(cw[:, 0, 0:1], 1.0).then_inc(S["tables_ready"], 1)


            def copy_ridx(t, d):
                if t.live(d, G):
                    wait_round(dve, back_in, t, d + RING, 64)
                    vec.tensor_copy(ridx[:, t.slot(d), :], column(id_s, t.i(d), t.fixed)).then_inc(S["ridx_ready"], 1)

            for j in range(AHEAD):
                copy_ridx(Turn(0, j), 0)

            def body2(t):
                steps = iter(())
                if t.live(3):
                    steps = chain(t, 3, TPG, st[:, t.slot(3, 2)], rs[:, t.slot(3, 2)], S["chain2"], S["edge_stats"],
                                  lambda: None)

                def more(n=1):
                    for _ in range(n):
                        next(steps, None)

                copy_ridx(t, -AHEAD)
                more()
                if t.live(0):
                    m = mx[:, t.slot(0, 2), :]
                    wait(dve, S["sb_ready"], t, 0)
                    wait(dve, S["dt_ready"], t, 2)
                    wait_round(dve, far_in, t, 0, 16)
                    if not (t.fixed and t.i(0) == 0):
                        vec.tensor_copy(m[:, 0:1], mx[:, t.slot(1, 2), GE:GE + 1])
                    vec.tensor_tensor_scan(m[:, 1:GE + 1], far[:, t.slot(), :], p_dt[:, 0, :],
                                           0.0 if t.fixed and t.i(0) == 0 else mx[:, t.slot(1, 2), GE:GE + 1],
                                           ALU.add, ALU.max).then_inc(S["m_ready"], 1)
                    more(2)
                if t.live(1):
                    pp = pa[:, t.slot(1, 2)]
                    wait(dve, S["pa_ready"], t, 1)
                    wait(dve, S["agg_ready"], t, 3)
                    vec.tensor_tensor_scan(den[:, t.slot(1, 2), :], pp[:, 1, :], pp[:, 0, :],
                                           den[:, t.slot(2, 2), GE - 1:GE], ALU.mult, ALU.add)
                    more(2)
                    wait(dve, S["mT_ready"], t, 1)
                    vec.tensor_tensor(v[:], pp[:, 0, :], p_w[:], ALU.mult).then_inc(S["v_ready"], 1)
                    more(3)
                    wait(dve, S["v_ready"], t, 1)
                    vec.tensor_tensor_scan(z[:, t.slot(1, 2), :], pp[:, 1, :], v[:], z[:, t.slot(2, 2), GE - 1:GE],
                                           ALU.mult, ALU.add).then_inc(S["z_ready"], 1)
                    more(2)
                if t.live(2):
                    wait(dve, S["agg_ready"], t, 2)
                    vec.tensor_scalar(rden[:, 0, :], p_2[:, 0:TPG], 2.0, 2 * EPS_DEN, ALU.mult, ALU.add
                                      ).then_inc(S["rden_ready"], 1)
                    more(1)
                    wait(dve, S["rden_ready"], t, 2, per=2, off=-1)
                    vec.reciprocal(rden[:, 1, :], rden[:, 0, :]).then_inc(S["rden_ready"], 1)
                    more(1)
                    wait(dve, S["rden_ready"], t, 2, per=2)
                    wait(dve, S["res_ready"], t, 4)
                    for q in range(TPG):
                        vec.scalar_tensor_tensor(out=yb[t.slot(2, 2)][:, q * H:(q + 1) * H], in0=p_m[:, q, :],
                                                 scalar=rden[:, 1, q:q + 1], in1=back[:, t.slot(2), q, 0:H],
                                                 op0=ALU.mult, op1=ALU.add).then_inc(S["y_done"], 1)
                        more(1)
                    for q in range(TPG):
                        wait(dve, S["y_done"], t, 2, per=TPG, off=q + 1 - TPG)
                        ins = vec.bn_stats(st[:, t.slot(2, 2), q, :], yb[t.slot(2, 2)][:, q * H:(q + 1) * H])
                        more(1)
                    ins.then_inc(S["edge_stats"], 1)
                more(99)
                if t.live(3):
                    wait_round(dve, scattered, t, 3 + RING, 64)
                    vec.tensor_copy(sidx[:, t.slot(3), :], column(sidx_t, t.i(3), t.fixed)).then_inc(S["sidx_ready"], 1)

            rounds(dve, body2, 1)


def kernel(x, src, dst, edge_attr_3, edge_weight1, node_vec, L0_gnn_W1, L0_gnn_b1, L0_gnn_W2, L0_gnn_b2, L0_gnn_W3,
           L0_gnn_b3, L0_gnn_Wv):
    import numpy as np
    import concourse.bacc as bacc
    from concourse import mybir as mb
    from concourse.bass_utils import run_bass_kernel_spmd

    src = np.asarray(src)
    dst = np.asarray(dst)
    rcv = np.full(EP, N, src.dtype)
    rcv[:E] = src
    snd = np.zeros(EP, dst.dtype)
    snd[:E] = dst
    ef = np.zeros((4, EP), np.float32)
    ef[0:3, :E] = np.asarray(edge_attr_3).T
    ef[3, :E] = np.asarray(edge_weight1)[:, 0]

    def nat(a):
        return np.ascontiguousarray(a.reshape(G * TPG, P).T)

    arrays = {
        "xw": np.concatenate([np.asarray(x), np.asarray(node_vec)[:, None]], axis=1),
        "snd_nat": nat(snd),
        "rcv_nat": nat(rcv),
        "id_nat": nat(np.arange(EP, dtype=np.float32)),
        "key_row": rcv.reshape(1, EP),
        "iota": np.arange(CH, dtype=np.float32).reshape(1, CH),
        "tri": np.triu(np.ones((P, P), np.float32), 1),
        "ef_t": ef,
        "w1": np.asarray(L0_gnn_W1),
        "b1": np.asarray(L0_gnn_b1).reshape(1, H),
        "w2": np.asarray(L0_gnn_W2),
        "b2": np.asarray(L0_gnn_b2).reshape(1, H),
        "w3": np.asarray(L0_gnn_W3),
        "b3": np.ascontiguousarray(np.broadcast_to(np.asarray(L0_gnn_b3).reshape(1, 1), (1, H))),
        "wv": np.asarray(L0_gnn_Wv),
        "eye": np.eye(P, dtype=np.float32),
    }
    nc = bacc.Bacc("TRN2", target_bir_lowering=False, num_devices=1)
    feed, args = {}, []
    for name, a in arrays.items():
        a = np.ascontiguousarray(a)
        feed[f"in_{name}"] = a
        args.append(nc.dram_tensor(f"in_{name}", a.shape, mb.dt.from_np(a.dtype), kind="ExternalInput").ap())
    out = nc.dram_tensor("out_rows", (N, H), mb.dt.float32, kind="ExternalOutput").ap()
    gnn_kernel(nc, *args, out)
    r = run_bass_kernel_spmd(nc, [feed], core_ids=[0])
    return r.results[0]["out_rows"]
```
